# Optimizing a Trainium2 kernel written in Bass

```python
import numpy as np
import jax
import jax.numpy as jnp

def _softmax(x, axis=-1):
    return jax.nn.softmax(x, axis=axis)

def _gelu(x):
    return jax.nn.gelu(x, approximate=True)

def _silu(x):
    return jax.nn.silu(x)

def _sigmoid(x):
    return jax.nn.sigmoid(x)

def _layernorm(x, axis=-1, eps=1e-05):
    m = jnp.mean(x, axis=axis, keepdims=True)
    v = jnp.var(x, axis=axis, keepdims=True)
    return (x - m) / jnp.sqrt(v + eps)

def _scatter_add(tgt, idx, src, axis=0):
    return tgt.at[idx].add(src)

def _segment_sum(src, seg, n):
    return jax.ops.segment_sum(src, seg, n)
kernel_name = 'mk_adaln_d1_jaxref_r8_420d3e'

def setup_inputs(seed: int=0):
    np.random.seed(seed)
    _w = jnp.asarray

    def _L0_attn_setup():
        import jax, jax.numpy as jnp
        import numpy as np
        B, S, D = (4, 512, 128)
        H = 8
        DK = D // H
        DV = D // H
        KLEPE = 5
        ROPE_BASE = 10000.0

        def rotate_half(x):
            x1, x2 = jnp.split(x, 2, axis=-1)
            return jnp.concatenate([-x2, x1], axis=-1)

        def rope_sin_cos(seq_len, dim):
            inv_freq = 1.0 / ROPE_BASE ** (jnp.arange(0, dim, 2, dtype=jnp.float32) / dim)
            freqs = jnp.arange(seq_len, dtype=jnp.float32)[:, None] * inv_freq[None, :]
            emb = jnp.concatenate([freqs, freqs], axis=-1)
            return (jnp.sin(emb), jnp.cos(emb))

        def mala_attn(q, k, v):
            sin, cos = rope_sin_cos(q.shape[1], q.shape[-1])
            sin, cos = (sin[None, :, None, :], cos[None, :, None, :])
            q = q * cos + rotate_half(q) * sin
            k = k * cos + rotate_half(k) * sin
            scale = q.shape[-1] ** (-0.5)
            seq_len = q.shape[1]
            kv = jnp.einsum('bshd,bshe->bhde', k, v)
            ksum = k.sum(axis=1)
            vsum = v.sum(axis=1)
            num = jnp.einsum('bshd,bhde->bshe', q, kv) * scale + vsum[:, None, :, :]
            den = jnp.einsum('bshd,bhd->bsh', q, ksum) * scale + seq_len
            return num / den[..., None]

        def lepe_conv(v, w, b):
            Bb, Ss = (v.shape[0], v.shape[1])
            x = v.transpose(0, 2, 3, 1).reshape(Bb, H * DV, Ss)
            y = jax.lax.conv_general_dilated(x, w, window_strides=(1,), padding=[(KLEPE // 2, KLEPE // 2)], dimension_numbers=('NCH', 'OIH', 'NCH'), feature_group_count=H * DV)
            y = y + b[None, :, None]
            return y.reshape(Bb, H, DV, Ss).transpose(0, 3, 1, 2)
        key = jax.random.key(seed)
        ks = jax.random.split(key, 8)
        w = 0.02
        return {'hidden_states': jax.random.normal(ks[0], (B, S, D), dtype=jnp.float32), 'Wq': jax.random.normal(ks[1], (D, D), dtype=jnp.float32) * w, 'Wk': jax.random.normal(ks[2], (D, D), dtype=jnp.float32) * w, 'Wv': jax.random.normal(ks[3], (D, D), dtype=jnp.float32) * w, 'Wg': jax.random.normal(ks[4], (D, D), dtype=jnp.float32) * w, 'Wo': jax.random.normal(ks[5], (D, D), dtype=jnp.float32) * w, 'lepe_w': jax.random.normal(ks[6], (D, 1, KLEPE), dtype=jnp.float32) * 0.1, 'lepe_b': jnp.zeros((D,), dtype=jnp.float32)}
    _L0_attn_in = _L0_attn_setup()

    def _L0_ffn_setup():
        import jax, jax.numpy as jnp
        import numpy as np
        B, S, D, H, E, K = (4, 256, 128, 256, 8, 2)
        TEMP = 5.0
        EPS = 1e-09
        key = jax.random.key(seed)
        k_x, k_wg, k_w1, k_w2 = jax.random.split(key, 4)
        scale = 0.02
        return {'x': jax.random.normal(k_x, (B, S, D), dtype=jnp.float32), 'Wg': jax.random.normal(k_wg, (D, E), dtype=jnp.float32) * scale, 'bg': jnp.zeros((E,), dtype=jnp.float32), 'W1': jax.random.normal(k_w1, (E, D, H), dtype=jnp.float32) * scale, 'b1': jnp.zeros((E, H), dtype=jnp.float32), 'W2': jax.random.normal(k_w2, (E, H, D), dtype=jnp.float32) * scale, 'b2': jnp.zeros((E, D), dtype=jnp.float32)}
    _L0_ffn_in = _L0_ffn_setup()
    _L0_c = _w((lambda *s: np.random.randn(*s).astype(np.float32) * 0.05)(8, 128))
    _L0_wmod = _w((lambda *s: np.random.randn(*s).astype(np.float32) * 0.05)(128, 6 * 128) * 128 ** (-0.5))
    _d = {'L0_attn_hidden_states': _L0_attn_in['hidden_states'], 'L0_attn_Wq': _L0_attn_in['Wq'], 'L0_attn_Wk': _L0_attn_in['Wk'], 'L0_attn_Wv': _L0_attn_in['Wv'], 'L0_attn_Wg': _L0_attn_in['Wg'], 'L0_attn_Wo': _L0_attn_in['Wo'], 'L0_attn_lepe_w': _L0_attn_in['lepe_w'], 'L0_attn_lepe_b': _L0_attn_in['lepe_b'], 'L0_ffn_Wg': _L0_ffn_in['Wg'], 'L0_ffn_bg': _L0_ffn_in['bg'], 'L0_ffn_W1': _L0_ffn_in['W1'], 'L0_ffn_b1': _L0_ffn_in['b1'], 'L0_ffn_W2': _L0_ffn_in['W2'], 'L0_ffn_b2': _L0_ffn_in['b2'], 'L0_c': _L0_c, 'L0_wmod': _L0_wmod}
    _x0 = _d['L0_attn_hidden_states']
    _d['L0_attn_hidden_states'] = jax.random.normal(jax.random.fold_in(jax.random.key(seed), 1), (8, 1024, 128), dtype=_x0.dtype)
    del _x0
    return _d

def reference(L0_attn_hidden_states, L0_attn_Wq, L0_attn_Wk, L0_attn_Wv, L0_attn_Wg, L0_attn_Wo, L0_attn_lepe_w, L0_attn_lepe_b, L0_ffn_Wg, L0_ffn_bg, L0_ffn_W1, L0_ffn_b1, L0_ffn_W2, L0_ffn_b2, L0_c, L0_wmod):

    def _L0_attn_ref(hidden_states, Wq, Wk, Wv, Wg, Wo, lepe_w, lepe_b):
        import jax, jax.numpy as jnp
        import numpy as np
        B, S, D = (4, 512, 128)
        H = 8
        DK = D // H
        DV = D // H
        KLEPE = 5
        ROPE_BASE = 10000.0

        def rotate_half(x):
            x1, x2 = jnp.split(x, 2, axis=-1)
            return jnp.concatenate([-x2, x1], axis=-1)

        def rope_sin_cos(seq_len, dim):
            inv_freq = 1.0 / ROPE_BASE ** (jnp.arange(0, dim, 2, dtype=jnp.float32) / dim)
            freqs = jnp.arange(seq_len, dtype=jnp.float32)[:, None] * inv_freq[None, :]
            emb = jnp.concatenate([freqs, freqs], axis=-1)
            return (jnp.sin(emb), jnp.cos(emb))

        def mala_attn(q, k, v):
            sin, cos = rope_sin_cos(q.shape[1], q.shape[-1])
            sin, cos = (sin[None, :, None, :], cos[None, :, None, :])
            q = q * cos + rotate_half(q) * sin
            k = k * cos + rotate_half(k) * sin
            scale = q.shape[-1] ** (-0.5)
            seq_len = q.shape[1]
            kv = jnp.einsum('bshd,bshe->bhde', k, v)
            ksum = k.sum(axis=1)
            vsum = v.sum(axis=1)
            num = jnp.einsum('bshd,bhde->bshe', q, kv) * scale + vsum[:, None, :, :]
            den = jnp.einsum('bshd,bhd->bsh', q, ksum) * scale + seq_len
            return num / den[..., None]

        def lepe_conv(v, w, b):
            Bb, Ss = (v.shape[0], v.shape[1])
            x = v.transpose(0, 2, 3, 1).reshape(Bb, H * DV, Ss)
            y = jax.lax.conv_general_dilated(x, w, window_strides=(1,), padding=[(KLEPE // 2, KLEPE // 2)], dimension_numbers=('NCH', 'OIH', 'NCH'), feature_group_count=H * DV)
            y = y + b[None, :, None]
            return y.reshape(Bb, H, DV, Ss).transpose(0, 3, 1, 2)
        Bb, Ss, _ = hidden_states.shape
        q = (hidden_states @ Wq.T).reshape(Bb, Ss, H, DK)
        k = (hidden_states @ Wk.T).reshape(Bb, Ss, H, DK)
        v = (hidden_states @ Wv.T).reshape(Bb, Ss, H, DV)
        o_gate = hidden_states @ Wg.T
        o = mala_attn(q, k, v) + lepe_conv(v, lepe_w, lepe_b)
        o = o.reshape(Bb, Ss, H * DV) * o_gate
        return o @ Wo.T

    def _L0_ffn_ref(x, Wg, bg, W1, b1, W2, b2):
        import jax, jax.numpy as jnp
        import numpy as np
        B, S, D, H, E, K = (4, 256, 128, 256, 8, 2)
        TEMP = 5.0
        EPS = 1e-09
        logits = jnp.einsum('bsd,de->bse', x, Wg) + bg
        probs = jax.nn.softmax(logits / TEMP, axis=-1)
        vals, idx = jax.lax.top_k(probs, K)
        onehot = jax.nn.one_hot(idx, E, dtype=x.dtype)
        mask = jnp.einsum('bske,bsk->bse', onehot, vals)
        gates = mask / (jnp.sum(mask, axis=-1, keepdims=True) + EPS)
        h = jax.nn.gelu(jnp.einsum('bsd,edh->besh', x, W1) + b1[None, :, None, :], approximate=False)
        out = jnp.einsum('besh,ehd->besd', h, W2) + b2[None, :, None, :]
        y = jnp.einsum('bse,besd->bsd', gates, out)
        return y
    x = L0_attn_hidden_states
    mod = (_silu(L0_c) @ L0_wmod).reshape(L0_c.shape[0], 6, 1, -1)
    sa, ca, ga, sb, cb, gb = (mod[:, 0], mod[:, 1], mod[:, 2], mod[:, 3], mod[:, 4], mod[:, 5])
    ga = (2 * (ga >= 0) - 1) * jnp.maximum(jnp.abs(ga), 0.25)
    gb = (2 * (gb >= 0) - 1) * jnp.maximum(jnp.abs(gb), 0.25)
    h = _layernorm(x, axis=-1) * (1 + ca) + sa
    x = x + ga * _L0_attn_ref(h, L0_attn_Wq, L0_attn_Wk, L0_attn_Wv, L0_attn_Wg, L0_attn_Wo, L0_attn_lepe_w, L0_attn_lepe_b)
    h = _layernorm(x, axis=-1) * (1 + cb) + sb
    x = x + gb * _L0_ffn_ref(h, L0_ffn_Wg, L0_ffn_bg, L0_ffn_W1, L0_ffn_b1, L0_ffn_W2, L0_ffn_b2)
    return x

_drawn_inputs = setup_inputs


def setup_inputs(seed=0):
    import zlib

    import numpy as np

    out = dict(_drawn_inputs(seed))
    spreads = {'L0_attn_lepe_b': (0.0, 0.8),
     'L0_ffn_bg': (0.0, 0.734),
     'L0_ffn_b1': (0.0, 0.8),
     'L0_ffn_b2': (0.0, 1.402)}
    factors = {'L0_attn_Wq': 8.0,
     'L0_attn_Wk': 8.0,
     'L0_attn_Wv': 8.0,
     'L0_attn_Wg': 8.0,
     'L0_attn_Wo': 8.0,
     'L0_attn_lepe_w': 8.0,
     'L0_ffn_Wg': 3.473,
     'L0_ffn_W1': 8.0,
     'L0_ffn_W2': 7.631,
     'L0_c': 2.993,
     'L0_wmod': 2.909}
    for name, (base, spread) in spreads.items():
        noise = np.random.default_rng([zlib.crc32(name.encode()), seed]).standard_normal(out[name].shape)
        drawn = base * np.exp(spread * noise) if base else spread * noise
        out[name] = jnp.asarray(drawn.astype(out[name].dtype))
    for name, factor in factors.items():
        out[name] = (out[name] * factor).astype(out[name].dtype)
    return out
```

```python
from contextlib import ExitStack

import concourse.bass as bass
from concourse import mybir

F32 = mybir.dt.float32
F32R = mybir.dt.float32r
ALU = mybir.AluOpType
ACT = mybir.ActivationFunctionType
AX_X = mybir.AxisListType.X

P = 128
B, S, D = 8, 1024, 128
HEADS, DK = 8, 16
TAPS = 5
PAD = TAPS // 2
E, HID = 8, 256
HH = HID // P
J = S // P
CH = 2
CT = S // CH
JC = CT // P
UNITS = CH * E
TEMP = 5.0
EPS_GATE = 1e-9
EPS_LN = 1e-5
KV = slice(D, 2 * D)

RING = 3
USES = ([("xT", c) for c in range(CH)] + [("qkv", j) for j in range(J)]
        + [("vT", c) for c in range(CH)] + [("kv", 0)] + [("qT", c) for c in range(CH)]
        + [("den", 0), ("num", 0), ("num", 1), ("rdenT", 0), ("rdenT", 1), ("gate", 0), ("gate", 1),
           ("out", 0), ("out", 1), ("x1T", 0), ("x1T", 1), ("logit", 0), ("logit", 1),
           ("logitT", 0), ("gatesT", 0)])
assert len(USES) % RING == 0
USE = {u: k for k, u in enumerate(USES)}

TICK = {0: ["norm1"], 1: ["xT"], 2: ["qkv0"], 3: ["qkv1"], 4: ["vT_kv"], 5: ["qT"], 6: ["den_num"],
        7: ["rdenT"], 8: ["gate"], 9: ["out0"], 10: ["out1"], 11: ["x1T"], 12: ["logits"],
        13: ["logitT"], 14: ["route"], 15: []}
STAGES = [s for k in range(UNITS) for s in TICK[k]]

SLOTS = list(range(E + 3)) + [("y", 0)] + list(range(E + 3, UNITS)) + [("y", 1)]
assert len(SLOTS) % 2 == 0
SLOT = {u: k for k, u in enumerate(SLOTS)}


class Step:

    def __init__(self, t, off):
        self.t, self.off = t, off
        self.par = off % 2

    def count(self, per, n=0):
        return self.t * (2 * per) + (self.off * per + n)

    def half(self, per, n=0):
        return self.t * per + ((self.off // 2) * per + n)

    def row(self):
        return bass.ds(self.t * 2 + self.off, 1)


def schedule(eng, attention, experts):
    for s in STAGES:
        attention(Step(0, 0), s)
    first = Step(0, 0)
    experts(first, Step(0, 1))
    with eng.Fori(0, (B - 2) // 2) as t:
        experts(Step(t, 1), Step(t, 2))
        experts(Step(t, 2), Step(t, 3))
    experts(Step(0, B - 1), None)


def adaln_moe_kernel(nc, x, wqkvg, wo, wmod, c_t, lepe, w_route, b_route, w1, b1, w2, b2, rope,
                     consts, out):
    with ExitStack() as ctx:
        def sb(name, shape, dt=F32):
            return ctx.enter_context(nc.sbuf_tensor(name, shape, dt))

        def ps(name, shape):
            return ctx.enter_context(nc.psum_tensor(name, shape, F32))

        def sem(name):
            return ctx.enter_context(nc.semaphore(name))

        space_a, space_b = sb("space_a", [P, E * HID]), sb("space_b", [P, 4 * D])
        w1_f = space_a[:, :].rearrange("p (e h) -> p e h", e=E)
        wqkvg_f = space_b[:, :]
        products = space_a[:, :].rearrange("p (k j d) -> p k j d", k=2, j=JC)
        qk_cos, qk_sin = products[:, 0], products[:, 1]
        wqkvg_h, wqkvg_l = sb("wqkvg_h", [P, 4 * D], F32R), sb("wqkvg_l", [P, 4 * D], F32R)
        wo_f = sb("wo_f", [P, D])
        wmod_f = sb("wmod_f", [P, 6 * D])
        cond = sb("cond", [P, B])
        silu = sb("silu", [P, B])
        lepe_f = sb("lepe_f", [P, TAPS + 1])
        wr_f = sb("wr_f", [P, P])
        wr_h, wr_l = sb("wr_h", [P, P], F32R), sb("wr_l", [P, P], F32R)
        br_f = sb("br_f", [E, 1])
        w1_h, w1_l = sb("w1_h", [P, E, HID], F32R), sb("w1_l", [P, E, HID], F32R)
        b1_f = sb("b1_f", [P, E, HH])
        w2_f = sb("w2_f", [P, E, HH, D])
        b2_f = sb("b2_f", [E, D])
        rope_f = sb("rope_f", [P, 2, J, DK])
        consts_f = sb("consts_f", [P, consts.shape[1]])
        ident = consts_f[:, 0:P]
        head_mask = consts_f[:, P:2 * P]
        head_cols = consts_f[:, 2 * P:2 * P + HEADS]
        lower = consts_f[:, 2 * P + HEADS:2 * P + HEADS + E * E]
        minus_half, eps_ln = sb("minus_half", [P, J]), sb("eps_ln", [P, J])
        scratch = sb("scratch", [P, 1])
        mod = sb("mod", [P, 6, B])
        mod_a, mod_b = sb("mod_a", [P, 6, B]), sb("mod_b", [P, 6, B])
        ga = sb("ga", [P, B, D])

        xs = [sb(f"xs{i}", [P, J, D]) for i in range(2)]
        stats = sb("stats", [P, J, 6])
        mean_var = sb("mean_var", [P, J, 2])
        var_eps = sb("var_eps", [P, J])
        rstd = sb("rstd", [P, J])
        xn = sb("xn", [P, J, D])
        modc = sb("modc", [P, 6])
        wo_g = sb("wo_g", [P, D])
        h_f = sb("h_f", [P, S])
        h1_h, h1_l = sb("h1_h", [P, S], F32R), sb("h1_l", [P, S], F32R)
        qk = sb("qk", [P, J, 2 * D])
        v = sb("v", [P, J, D + 1])
        v_t = sb("v_t", [P, S + 2 * PAD])
        v_sums = sb("v_sums", [P, CH])
        v_sum = sb("v_sum", [P, 1])
        conv = sb("conv", [P, S])
        kv_s = sb("kv_s", [P, D])
        ksum_s = sb("ksum_s", [P, HEADS])
        q_t = xn[:, :, :].rearrange("p j d -> p (j d)")
        den = sb("den", [P, J * HEADS])
        rden = sb("rden", [P, J * HEADS])
        rden_x = sb("rden_x", [P, J * HEADS, DK])
        heads = sb("heads", [P, S])
        logit_t = conv[0:E, :]
        logit = sb("logit", [P, J, E])
        top = sb("top", [P, J])
        below = sb("below", [P, J, E])
        th = sb("th", [P, J, E])
        one_plus, one_minus = sb("one_plus", [P, J, E]), sb("one_minus", [P, J, E])
        inv_minus = sb("inv_minus", [P, J, E])
        root = sb("root", [P, J, E])
        power = sb("power", [P, J, E])
        z = sb("z", [P, J])
        rz = sb("rz", [P, J])
        prob = sb("prob", [P, J, E])
        lead = sb("lead", [P, J * E, E])
        tied = sb("tied", [P, J, E * E])
        rank = sb("rank", [P, J, E])
        chosen = sb("chosen", [P, J, E])
        masked = sb("masked", [P, J, E])
        total = sb("total", [P, J])
        total_eps = sb("total_eps", [P, J])
        r_total = sb("r_total", [P, J])
        gates = sb("gates", [P, E, J])
        gates_t = sb("gates_t", [E * J, P])

        x1 = [sb(f"x1_{i}", [P, J, D]) for i in range(2)]
        gb_c = [sb(f"gb_c{i}", [P, 1]) for i in range(2)]
        h2_h = [sb(f"h2_h{i}", [P, S], F32R) for i in range(2)]
        h2_l = [sb(f"h2_l{i}", [P, S], F32R) for i in range(2)]
        gates_dram = [nc.dram_tensor(f"gates_dram{i}", (E, S), F32, kind="Internal").ap() for i in range(2)]
        gates_e = [sb(f"gates_e{i}", [E, S]) for i in range(2)]
        gates_all = [sb(f"gates_all{c}", [P, E, CT]) for c in range(CH)]

        hid = [sb(f"hid{i}", [P, HH, CT]) for i in range(2)]
        hid_g = [sb(f"hid_g{i}", [P, HH, CT]) for i in range(4)]
        y_t = sb("y_t", [P, CT])
        y = [sb(f"y{c}", [P, JC, D]) for c in range(CH)]

        ring = [ps(f"ring{i}", [P, 512]) for i in range(RING)]
        ps_h = [ps(f"ps_h{i}", [P, HH, CT]) for i in range(2)]
        ps_y = ps("ps_y", [P, CT])

        s_w = {k: sem(f"s_w_{k}") for k in ("attn", "mod", "small", "w1", "w2")}
        s_set = sem("s_set")
        s_silu = sem("s_silu")
        s_mod_ps = sem("s_mod_ps")
        s_mod = sem("s_mod")
        s_chain = sem("s_chain")
        s_x = [sem(f"s_xload{i}") for i in range(2)]
        s_stats = sem("s_stats")
        s_mv = sem("s_mv")
        s_veps = sem("s_veps")
        s_rstd = sem("s_rstd")
        s_xn = sem("s_xn")
        s_modc = sem("s_modc")
        s_xT = sem("s_xT")
        s_h1 = sem("s_h1")
        s_h1l = sem("s_h1l")
        s_qkv = sem("s_qkv")
        s_rot = sem("s_rot")
        s_v = sem("s_v")
        s_qk = sem("s_qk")
        s_vT = sem("s_vT")
        s_vt = sem("s_vt")
        s_vsum = sem("s_vsum")
        s_conv = sem("s_conv")
        s_kv = sem("s_kv")
        s_kvs = sem("s_kvs")
        s_qT = sem("s_qT")
        s_qt = sem("s_qt")
        s_den = sem("s_den")
        s_dens = sem("s_dens")
        s_rden = sem("s_rden")
        s_rdx = sem("s_rdx")
        s_num = sem("s_num")
        s_nums = sem("s_nums")
        s_rdT = sem("s_rdT")
        s_attn = sem("s_attn")
        s_mixed = sem("s_mixed")
        s_gate = sem("s_gate")
        s_ot = sem("s_ot")
        s_out = sem("s_out")
        s_x1 = sem("s_x1")
        s_x1T = sem("s_x1T")
        s_h2 = sem("s_h2")
        s_h2l = sem("s_h2l")
        s_lg = sem("s_lg")
        s_lgs = sem("s_lgs")
        s_lgT = sem("s_lgT")
        s_logit = sem("s_logit")
        s_top = sem("s_top")
        s_th = sem("s_th")
        s_lead = sem("s_lead")
        s_gates = sem("s_gates")
        s_gT = sem("s_gT")
        s_gts = sem("s_gts")
        s_gd = sem("s_gd")
        s_ge = sem("s_ge")
        s_gall = [sem(f"s_gall{c}") for c in range(CH)]
        s_l1 = sem("s_l1")
        s_gelu = sem("s_gelu")
        s_hg = sem("s_hg")
        s_l2 = sem("s_l2")
        s_yt = sem("s_yt")
        s_yT = sem("s_yT")
        s_y = sem("s_y")
        s_store = [sem(f"s_store{c}") for c in range(CH)]

        N_SET = 4 + 3 * 2
        ROUTE = 17

        READ = {}
        for c in range(CH):
            READ["xT", c] = (s_h1, CH, c + 1)
            READ["vT", c] = (s_vt, CH, c + 1)
            READ["qT", c] = (s_qt, CH, c + 1)
            READ["num", c] = (s_nums, CH, c + 1)
            READ["rdenT", c] = (s_attn, CH, c + 1)
            READ["gate", c] = (s_ot, CH, c + 1)
            READ["out", c] = (s_x1, CH, c + 1)
            READ["x1T", c] = (s_h2, CH, c + 1)
            READ["logit", c] = (s_lgs, CH, c + 1)
        for j in range(J):
            READ["qkv", j] = (s_v, J, j + 1)
        READ["kv", 0] = (s_kvs, 1, 1)
        READ["den", 0] = (s_dens, 1, 1)
        READ["logitT", 0] = (s_logit, 1, 1)
        READ["gatesT", 0] = (s_gts, 1, 1)

        def ring_of(name, c=0):
            return ring[USE[name, c] % RING]

        def bank_free(eng, step, name, c=0):
            k = USE[name, c] - RING
            if k < 0 and step.off == 0:
                return
            s_read, per, n = READ[USES[k]]
            eng.wait_ge(s_read, step.count(per, n if k >= 0 else n - per))

        def hidden_free(eng, step, slot):
            if slot < 2 and step.off == 0:
                return
            before = SLOTS[slot - 2]
            back = UNITS if slot < 2 else 0
            if isinstance(before, tuple):
                eng.wait_ge(s_y, step.count(CH, before[1] + 1 - (CH if back else 0)))
            else:
                eng.wait_ge(s_gelu, step.count(UNITS, before + 1 - back))

        block = ctx.enter_context(nc.Block())

        @block.sync
        def _(sp):
            def load_x(b):
                if b.off >= 2:
                    sp.wait_ge(s_x1, b.count(CH, -CH))
                sp.dma_start(xs[b.par][:, :, :], x[b.row()].rearrange("a (j p) d -> p (a j) d", p=P))\
                    .then_inc(s_x[b.par], 16)

            def spread_gates(b, c):
                if b.off >= 1:
                    sp.wait_ge(s_hg, b.count(UNITS, E * (c + 1) - UNITS))
                sp.dma_start(gates_all[c][:, :, :],
                             gates_dram[b.par][:, c * CT:(c + 1) * CT].partition_broadcast(P))\
                    .then_inc(s_gall[c], 16)

            def gates_out(b):
                sp.wait_ge(s_gts, b.count(1, 1))
                if b.off >= 2:
                    sp.wait_ge(s_gall[1], b.count(16, -16))
                sp.dma_start(gates_dram[b.par].rearrange("e (j t) -> (e j) t", t=P), gates_t[:, :])\
                    .then_inc(s_gd, 16)
                sp.wait_ge(s_gd, b.count(16, 16))
                if b.off >= 2:
                    sp.wait_ge(s_l2, b.count(UNITS, -UNITS))
                sp.dma_start(gates_e[b.par][:, :], gates_dram[b.par]).then_inc(s_ge, 16)
                spread_gates(b, 0)

            def store(f, c, back=0):
                row = bass.ds(f.t * 2 + (f.off - back), 1)
                sp.wait_ge(s_y, f.count(CH, c + 1 - CH * back))
                sp.dma_start(out[row][:, c * CT:(c + 1) * CT].rearrange("a (j p) d -> p (a j) d", p=P),
                             y[c][:, :, :]).then_inc(s_store[c], 16)

            def experts(f, b):
                if b is not None:
                    load_x(b)
                spread_gates(f, 1)
                if f.off >= 1:
                    store(f, 1, back=1)
                store(f, 0)
                if b is not None:
                    gates_out(b)

            first = Step(0, 0)
            load_x(first)
            sp.dma_start(cond[:, :], c_t).then_inc(s_w["mod"], 16)
            sp.dma_start(wmod_f[:, :], wmod).then_inc(s_w["mod"], 16)
            sp.dma_start(wqkvg_f, wqkvg).then_inc(s_w["attn"], 16)
            sp.dma_start(consts_f[:, :], consts).then_inc(s_w["small"], 16)
            sp.dma_start(rope_f[:, :, :, :], rope).then_inc(s_w["small"], 16)
            sp.dma_start(wo_f[:, :], wo).then_inc(s_w["small"], 16)
            sp.dma_start(lepe_f[:, :], lepe).then_inc(s_w["small"], 16)
            sp.dma_start(wr_f[:, 0:E], w_route).then_inc(s_w["small"], 16)
            sp.dma_start(br_f[:, :], b_route).then_inc(s_w["small"], 16)
            sp.dma_start(b2_f[:, :], b2).then_inc(s_w["small"], 16)
            sp.dma_start(b1_f[:, :, :], b1).then_inc(s_w["small"], 16)
            sp.dma_start(w1_f, w1).then_inc(s_w["w1"], 16)
            sp.dma_start(w2_f[:, :, :, :], w2).then_inc(s_w["w2"], 16)
            gates_out(first)
            experts(first, Step(0, 1))
            with sp.Fori(0, (B - 2) // 2) as t:
                experts(Step(t, 1), Step(t, 2))
                experts(Step(t, 2), Step(t, 3))
            experts(Step(0, B - 1), None)
            store(Step(0, B - 1), 1)
            for c in range(CH):
                sp.wait_ge(s_store[c], 16 * B)

        @block.tensor
        def _(pe):
            def transposes(dst, src, sem_):
                for j in range(JC):
                    last = pe.transpose(dst[:, j * P:(j + 1) * P], src(j), ident)
                last.then_inc(sem_, 1)

            def split(dst, wh, wl, ah, al):
                pe.matmul(dst, wh, ah, start=True, stop=False)
                pe.matmul(dst, wl, ah, start=False, stop=False)
                return pe.matmul(dst, wh, al, start=False, stop=True)

            def stage(b, name):
                if name == "xT":
                    for c in range(CH):
                        pe.wait_ge(s_xn, b.count(4, c + 1))
                        bank_free(pe, b, "xT", c)
                        transposes(ring_of("xT", c), lambda j: xn[:, c * JC + j, :], s_xT)
                elif name in ("qkv0", "qkv1"):
                    c = int(name[-1])
                    pe.wait_ge(s_h1l, b.count(2, c + 1))
                    for j in range(c * JC, (c + 1) * JC):
                        bank_free(pe, b, "qkv", j)
                        t = slice(j * P, (j + 1) * P)
                        w = slice(0, 3 * D)
                        split(ring_of("qkv", j)[:, w], h1_h[:, t], h1_l[:, t], wqkvg_h[:, w],
                              wqkvg_l[:, w]).then_inc(s_qkv, 1)
                elif name == "vT_kv":
                    pe.wait_ge(s_v, b.count(J, J))
                    for c in range(CH):
                        transposes(ring_of("vT", c), lambda j: v[:, c * JC + j, 0:D], s_vT)
                    pe.wait_ge(s_qk, b.count(J, J))
                    bank_free(pe, b, "kv")
                    for j in range(J):
                        last = pe.matmul(ring_of("kv")[:, 0:D + 1], qk[:, j, KV], v[:, j, :],
                                         start=(j == 0), stop=(j == J - 1))
                    last.then_inc(s_kv, 1)
                elif name == "qT":
                    for c in range(CH):
                        bank_free(pe, b, "qT", c)
                        transposes(ring_of("qT", c), lambda j: qk[:, c * JC + j, 0:D], s_qT)
                elif name == "den_num":
                    pe.wait_ge(s_kvs, b.count(1, 1))
                    pe.wait_ge(s_qt, b.count(2, 2))
                    bank_free(pe, b, "den")
                    for j in range(J):
                        last = pe.matmul(ring_of("den")[:, j * HEADS:(j + 1) * HEADS],
                                         q_t[:, j * P:(j + 1) * P], ksum_s[:, :], start=True, stop=True)
                    last.then_inc(s_den, 1)
                    for c in range(CH):
                        bank_free(pe, b, "num", c)
                        pe.matmul(ring_of("num", c)[:, :], kv_s[:, :], q_t[:, c * CT:(c + 1) * CT],
                                  start=True, stop=True).then_inc(s_num, 1)
                elif name == "rdenT":
                    for c in range(CH):
                        pe.wait_ge(s_rdx, b.count(2, c + 1))
                        bank_free(pe, b, "rdenT", c)
                        transposes(ring_of("rdenT", c),
                                   lambda j: rden_x[:, (c * JC + j) * HEADS:(c * JC + j + 1) * HEADS, :]
                                   .rearrange("p h d -> p (h d)"), s_rdT)
                elif name == "gate":
                    for c in range(CH):
                        bank_free(pe, b, "gate", c)
                        t = slice(c * CT, (c + 1) * CT)
                        w = slice(3 * D, 4 * D)
                        split(ring_of("gate", c)[:, :], wqkvg_h[:, w], wqkvg_l[:, w], h1_h[:, t],
                              h1_l[:, t]).then_inc(s_gate, 1)
                elif name in ("out0", "out1"):
                    c = int(name[-1])
                    pe.wait_ge(s_modc, b.count(3, 3))
                    pe.wait_ge(s_ot, b.count(2, c + 1))
                    if c == 0:
                        bank_free(pe, b, "out", c)
                    for j in range(JC):
                        t = c * JC + j
                        last = pe.matmul(ring_of("out", c)[:, j * P:(j + 1) * P],
                                         heads[:, t * P:(t + 1) * P], wo_g[:, :], start=True, stop=True)
                    last.then_inc(s_out, 1)
                elif name == "x1T":
                    for c in range(CH):
                        pe.wait_ge(s_xn, b.count(4, c + 3))
                        bank_free(pe, b, "x1T", c)
                        transposes(ring_of("x1T", c), lambda j: xn[:, c * JC + j, :], s_x1T)
                elif name == "logits":
                    for c in range(CH):
                        t = slice(c * CT, (c + 1) * CT)
                        pe.wait_ge(s_h2l, b.count(2, c + 1))
                        bank_free(pe, b, "logit", c)
                        split(ring_of("logit", c)[:, :], wr_h[:, :], wr_l[:, :], h2_h[b.par][:, t],
                              h2_l[b.par][:, t]).then_inc(s_lg, 1)
                elif name == "logitT":
                    pe.wait_ge(s_lgs, b.count(2, 2))
                    bank_free(pe, b, "logitT")
                    for j in range(J):
                        last = pe.matmul(ring_of("logitT")[:, j * E:(j + 1) * E],
                                         logit_t[:, j * P:(j + 1) * P], ident[0:E, 0:E],
                                         start=True, stop=True)
                    last.then_inc(s_lgT, 1)
                elif name == "route":
                    pe.wait_ge(s_gates, b.count(1, 1))
                    bank_free(pe, b, "gatesT")
                    pe.matmul(ring_of("gatesT")[0:E * J, 0:P], gates[:, :, :].rearrange("p e j -> p (e j)"),
                              ident, start=True, stop=True).then_inc(s_gT, 1)

            def layer1(f, n):
                c, e = divmod(n, E)
                slot = SLOT[n]
                hidden_free(pe, f, slot)
                t = slice(c * CT, (c + 1) * CT)
                for g in range(HH):
                    w = slice(g * P, (g + 1) * P)
                    last = split(ps_h[slot % 2][:, g, :], w1_h[:, e, w], w1_l[:, e, w],
                                 h2_h[f.par][:, t], h2_l[f.par][:, t])
                last.then_inc(s_l1, 1)

            def layer2(f, n):
                c, e = divmod(n, E)
                if e == 0:
                    pe.wait_ge(s_yt, f.count(2, c))
                    pe.wait_ge(s_ge, f.count(16, 16))
                    pe.matmul(ps_y[:, :], b2_f[:, :], gates_e[f.par][:, c * CT:(c + 1) * CT],
                              start=True, stop=False)
                pe.wait_ge(s_hg, f.count(UNITS, n + 1))
                for g in range(HH):
                    last = pe.matmul(ps_y[:, :], w2_f[:, e, g, :], hid_g[n % 4][:, g, :], start=False,
                                     stop=(e == E - 1 and g == HH - 1))
                last.then_inc(s_l2, 1)

            def turn_y(f, c):
                slot = SLOT["y", c]
                pe.wait_ge(s_yt, f.count(2, c + 1))
                hidden_free(pe, f, slot)
                transposes(ps_h[slot % 2][:, 0, :], lambda j: y_t[:, j * P:(j + 1) * P], s_yT)

            def experts(f, b):
                for n in range(UNITS):
                    layer1(f, n)
                    if b is not None:
                        for name in TICK[n]:
                            stage(b, name)
                    if n >= 2:
                        layer2(f, n - 2)
                    if n == E + 2:
                        turn_y(f, 0)
                layer2(f, UNITS - 2)
                layer2(f, UNITS - 1)
                turn_y(f, 1)

            pe.wait_ge(s_w["mod"], 32)
            pe.wait_ge(s_silu, 1)
            for m in range(6):
                pe.matmul(ring[0][:, m * B:(m + 1) * B], wmod_f[:, m * D:(m + 1) * D], silu[:, :],
                          start=True, stop=True)
            for r in range(B):
                last = pe.matmul(ps_h[0][:, r * D // CT, r * D % CT:r * D % CT + D],
                                 silu[:, r:r + 1].to_broadcast([P, P]), wmod_f[:, 2 * D:3 * D],
                                 start=True, stop=True)
            last.then_inc(s_mod_ps, 1)
            pe.wait_ge(s_set, N_SET)
            pe.wait_ge(s_w["small"], 8 * 16)
            pe.wait_ge(s_w["w2"], 16)
            pe.wait_ge(s_mod, 3)
            schedule(pe, stage, experts)

        @block.scalar
        def _(act):
            def stage(b, name):
                if name == "xT":
                    act.wait_ge(s_modc, b.count(3, 1))
                    for c in range(CH):
                        act.wait_ge(s_xT, b.count(CH, c + 1))
                        t = slice(c * CT, (c + 1) * CT)
                        act.activation(h1_h[:, t], ring_of("xT", c)[:, :], ACT.Identity,
                                       bias=modc[:, 0:1], scale=modc[:, 1:2])
                        act.activation(h_f[:, t], ring_of("xT", c)[:, :], ACT.Identity,
                                       bias=modc[:, 0:1], scale=modc[:, 1:2]).then_inc(s_h1, 1)
                elif name in ("qkv0", "qkv1"):
                    c = int(name[-1])
                    for j in range(c * JC, (c + 1) * JC):
                        act.wait_ge(s_rot, b.count(J, j + 1))
                        act.activation(v[:, j, 0:D], ring_of("qkv", j)[:, 2 * D:3 * D], ACT.Copy)\
                            .then_inc(s_v, 1)
                elif name == "vT_kv":
                    for c in range(CH):
                        act.wait_ge(s_vT, b.count(CH, c + 1))
                        act.activation(v_t[:, PAD + c * CT:PAD + (c + 1) * CT], ring_of("vT", c)[:, :],
                                       ACT.Identity, accum_out=v_sums[:, c:c + 1]).then_inc(s_vt, 1)
                elif name == "qT":
                    for c in range(CH):
                        act.wait_ge(s_qT, b.count(CH, c + 1))
                        act.activation(q_t[:, c * CT:(c + 1) * CT], ring_of("qT", c)[:, :],
                                       ACT.Copy).then_inc(s_qt, 1)
                elif name == "den_num":
                    act.wait_ge(s_vsum, b.count(1, 1))
                    for c in range(CH):
                        act.wait_ge(s_num, b.count(CH, c + 1))
                        act.activation(heads[:, c * CT:(c + 1) * CT], ring_of("num", c)[:, :],
                                       ACT.Identity, bias=v_sum[:, 0:1]).then_inc(s_nums, 1)
                    act.wait_ge(s_rden, b.count(1, 1))
                    for c in range(CH):
                        h = slice(c * JC * HEADS, (c + 1) * JC * HEADS)
                        act.activation(rden_x[:, h, :],
                                       rden[:, h].unsqueeze(2).to_broadcast([P, JC * HEADS, DK]),
                                       ACT.Copy).then_inc(s_rdx, 1)
                elif name == "x1T":
                    for c in range(CH):
                        act.wait_ge(s_x1T, b.count(CH, c + 1))
                        t = slice(c * CT, (c + 1) * CT)
                        act.activation(h2_h[b.par][:, t], ring_of("x1T", c)[:, :], ACT.Identity,
                                       bias=modc[:, 3:4], scale=modc[:, 4:5])
                        act.activation(h_f[:, t], ring_of("x1T", c)[:, :], ACT.Identity,
                                       bias=modc[:, 3:4], scale=modc[:, 4:5]).then_inc(s_h2, 1)
                elif name == "logits":
                    for c in range(CH):
                        act.wait_ge(s_lg, b.count(CH, c + 1))
                        act.activation(logit_t[:, c * CT:(c + 1) * CT], ring_of("logit", c)[0:E, :],
                                       ACT.Identity, bias=br_f[:, 0:1]).then_inc(s_lgs, 1)
                elif name == "logitT":
                    act.wait_ge(s_lgT, b.count(1, 1))
                    act.activation(logit[:, :, :].rearrange("p j e -> p (j e)"),
                                   ring_of("logitT")[:, 0:J * E], ACT.Copy).then_inc(s_logit, 1)
                elif name == "route":
                    act.wait_ge(s_top, b.count(ROUTE, 2))
                    act.activation(th[:, :, :], below[:, :, :], ACT.Tanh, scale=0.25 / TEMP)\
                        .then_inc(s_th, 1)
                    act.wait_ge(s_gT, b.count(1, 1))
                    if b.off >= 1:
                        act.wait_ge(s_gd, b.count(16, 0))
                    act.activation(gates_t[:, :], ring_of("gatesT")[0:E * J, 0:P], ACT.Copy)\
                        .then_inc(s_gts, 1)

            def gelu(f, n):
                e = n % E
                act.wait_ge(s_l1, f.count(UNITS, n + 1))
                if f.off >= 1 or n >= 2:
                    act.wait_ge(s_hg, f.count(UNITS, n - 1))
                for g in range(HH):
                    last = act.activation(hid[n % 2][:, g, :], ps_h[SLOT[n] % 2][:, g, :], ACT.Gelu,
                                          bias=b1_f[:, e, g:g + 1])
                last.then_inc(s_gelu, 1)

            def take_y(f, c):
                act.wait_ge(s_l2, f.count(UNITS, E * (c + 1)))
                act.activation(y_t[:, :], ps_y[:, :], ACT.Identity, scale=gb_c[f.par][:, 0:1])\
                    .then_inc(s_yt, 1)

            def experts(f, b):
                for n in range(UNITS):
                    gelu(f, n)
                    if b is not None:
                        for name in TICK[n]:
                            stage(b, name)
                    if n == E + 1:
                        take_y(f, 0)
                take_y(f, 1)

            act.wait_ge(s_w["mod"], 32)
            act.activation(silu[:, :], cond[:, :], ACT.Silu).then_inc(s_silu, 1)
            act.wait_ge(s_w["small"], 8 * 16)
            schedule(act, stage, experts)

        @block.gpsimd
        def _(pool):
            def deviation(b, n):
                pool.wait_ge(s_mv, b.count(2, n + 1))
                pool.tensor_tensor(var_eps[:, :], mean_var[:, :, 1], eps_ln[:, :], ALU.add)\
                    .then_inc(s_veps, 1)
                pool.wait_ge(s_veps, b.count(2, n + 1))
                pool.tensor_tensor(rstd[:, :], var_eps[:, :], minus_half[:, :], ALU.pow)\
                    .then_inc(s_rstd, 1)

            def stage(b, name):
                if name == "norm1":
                    deviation(b, 0)
                elif name in ("qkv0", "qkv1"):
                    c = int(name[-1])
                    for j in range(c * JC, (c + 1) * JC):
                        pool.wait_ge(s_rot, b.count(J, j + 1))
                        pool.tensor_tensor(qk[:, j, :], qk_cos[:, j % JC, :], qk_sin[:, j % JC, :], ALU.add)\
                            .then_inc(s_qk, 1)
                elif name == "rdenT":
                    pool.wait_ge(s_conv, b.count(TAPS, TAPS))
                    for c in range(CH):
                        pool.wait_ge(s_attn, b.count(CH, c + 1))
                        t = slice(c * CT, (c + 1) * CT)
                        pool.tensor_tensor(heads[:, t], heads[:, t], conv[:, t], ALU.add)\
                            .then_inc(s_mixed, 1)
                elif name == "out1":
                    deviation(b, 1)
                elif name == "logitT":
                    pool.wait_ge(s_logit, b.count(1, 1))
                    pool.tensor_tensor(lead[:, :, :].rearrange("p (j e) f -> p j e f", e=E),
                                       logit[:, :, :].unsqueeze(2).to_broadcast([P, J, E, E]),
                                       logit[:, :, :].unsqueeze(3).to_broadcast([P, J, E, E]),
                                       ALU.subtract).then_inc(s_lead, 1)

            def experts(f, b):
                if b is not None:
                    for n in range(UNITS):
                        for name in TICK[n]:
                            stage(b, name)

            pool.wait_ge(s_set, N_SET)
            pool.wait_ge(s_w["small"], 8 * 16)
            schedule(pool, stage, experts)

        @block.vector
        def _(dve):
            def statistics(b, src, n):
                for j in range(J):
                    last = dve.bn_stats(stats[:, j, :], src[:, j, :])
                last.then_inc(s_stats, 1)
                dve.wait_ge(s_stats, b.count(2, n + 1))
                dve.memset(scratch[:, :], 0.0)
                for j in range(J):
                    last = dve.bn_aggr(mean_var[:, j, :], stats[:, j, :])
                last.then_inc(s_mv, 1)

            def normalise(b, src, n):
                dve.wait_ge(s_rstd, b.count(2, n + 1))
                for j in range(J):
                    last = dve.tensor_scalar(xn[:, j, :], src[:, j, :], mean_var[:, j, 0:1],
                                             rstd[:, j:j + 1], ALU.subtract, ALU.mult)
                    if j % JC == JC - 1:
                        last.then_inc(s_xn, 1)

            def halves(ap, groups=2 * HEADS):
                return ap.rearrange("p (g h d) -> p g h d", h=2, d=DK // 2)

            def table(k, j):
                return halves(rope_f[:, k, j, :]).to_broadcast([P, 2 * HEADS, 2, DK // 2])

            def stage(b, name):
                if name == "norm1":
                    if b.off == 0:
                        modulation()
                    dve.tensor_copy(modc[:, :].unsqueeze(2), mod[:, :, b.row()]).then_inc(s_modc, 1)
                    dve.tensor_copy(gb_c[b.par][:, :].unsqueeze(2), mod[:, 5:6, b.row()])\
                        .then_inc(s_modc, 1)
                    dve.tensor_tensor(wo_g[:, :].unsqueeze(1), wo_f[:, :].unsqueeze(1),
                                      ga[:, b.row(), :], ALU.mult).then_inc(s_modc, 1)
                    dve.wait_ge(s_x[b.par], b.half(16, 16))
                    statistics(b, xs[b.par], 0)
                elif name == "xT":
                    normalise(b, xs[b.par], 0)
                    for c in range(CH):
                        dve.wait_ge(s_h1, b.count(CH, c + 1))
                        t = slice(c * CT, (c + 1) * CT)
                        dve.tensor_tensor(h1_l[:, t], h_f[:, t], h1_h[:, t].bitcast(F32),
                                          ALU.subtract).then_inc(s_h1l, 1)
                elif name in ("qkv0", "qkv1"):
                    c = int(name[-1])
                    for j in range(c * JC, (c + 1) * JC):
                        dve.wait_ge(s_qkv, b.count(J, j + 1))
                        if j >= JC:
                            dve.wait_ge(s_qk, b.count(J, j - JC + 1))
                        src = halves(ring_of("qkv", j)[:, 0:2 * D])
                        dve.tensor_tensor(halves(qk_cos[:, j % JC, :]), src, table(0, j), ALU.mult)
                        dve.tensor_tensor(halves(qk_sin[:, j % JC, :]), src[:, :, ::-1, :], table(1, j),
                                          ALU.mult).then_inc(s_rot, 1)
                elif name == "vT_kv":
                    dve.wait_ge(s_vt, b.count(CH, CH))
                    dve.tensor_tensor(v_sum[:, :], v_sums[:, 0:1], v_sums[:, 1:2], ALU.add)\
                        .then_inc(s_vsum, 1)
                    dve.wait_ge(s_kv, b.count(1, 1))
                    dve.tensor_tensor(kv_s[:, :], ring_of("kv")[:, 0:D], head_mask, ALU.mult)
                    dve.tensor_scalar(ksum_s[:, :], head_cols, ring_of("kv")[:, D:D + 1], None,
                                      ALU.mult).then_inc(s_kvs, 1)
                    dve.tensor_scalar(conv[:, :], v_t[:, 0:S], lepe_f[:, 0:1], lepe_f[:, TAPS:TAPS + 1],
                                      ALU.mult, ALU.add).then_inc(s_conv, 1)
                    for k in range(1, TAPS):
                        dve.wait_ge(s_conv, b.count(TAPS, k))
                        dve.scalar_tensor_tensor(conv[:, :], v_t[:, k:k + S], lepe_f[:, k:k + 1],
                                                 conv[:, :], ALU.mult, ALU.add).then_inc(s_conv, 1)
                elif name == "den_num":
                    dve.wait_ge(s_den, b.count(1, 1))
                    dve.tensor_scalar(den[:, :], ring_of("den")[:, 0:J * HEADS], float(S), None,
                                      ALU.add).then_inc(s_dens, 1)
                    dve.wait_ge(s_dens, b.count(1, 1))
                    dve.reciprocal(rden[:, :], den[:, :]).then_inc(s_rden, 1)
                elif name == "rdenT":
                    for c in range(CH):
                        dve.wait_ge(s_nums, b.count(CH, c + 1))
                        dve.wait_ge(s_rdT, b.count(CH, c + 1))
                        t = slice(c * CT, (c + 1) * CT)
                        dve.tensor_tensor(heads[:, t], heads[:, t], ring_of("rdenT", c)[:, :], ALU.mult)\
                            .then_inc(s_attn, 1)
                elif name == "gate":
                    for c in range(CH):
                        dve.wait_ge(s_mixed, b.count(CH, c + 1))
                        dve.wait_ge(s_gate, b.count(CH, c + 1))
                        t = slice(c * CT, (c + 1) * CT)
                        dve.tensor_tensor(heads[:, t], heads[:, t], ring_of("gate", c)[:, :], ALU.mult)\
                            .then_inc(s_ot, 1)
                elif name in ("out0", "out1"):
                    c = int(name[-1])
                    dve.wait_ge(s_out, b.count(CH, c + 1))
                    j = slice(c * JC, (c + 1) * JC)
                    dve.tensor_tensor(x1[b.par][:, j, :], xs[b.par][:, j, :],
                                      ring_of("out", c)[:, :].rearrange("p (j d) -> p j d", d=D),
                                      ALU.add).then_inc(s_x1, 1)
                    if c == CH - 1:
                        dve.wait_ge(s_x1, b.count(CH, CH))
                        statistics(b, x1[b.par], 1)
                elif name == "x1T":
                    normalise(b, x1[b.par], 1)
                    for c in range(CH):
                        dve.wait_ge(s_h2, b.count(CH, c + 1))
                        t = slice(c * CT, (c + 1) * CT)
                        dve.tensor_tensor(h2_l[b.par][:, t], h_f[:, t], h2_h[b.par][:, t].bitcast(F32),
                                          ALU.subtract).then_inc(s_h2l, 1)
                elif name == "logitT":
                    dve.wait_ge(s_logit, b.count(1, 1))
                    step(b, 1, dve.tensor_reduce(top[:, :], logit[:, :, :], AX_X, ALU.max))
                    step(b, 2, dve.tensor_tensor(below[:, :, :], logit[:, :, :],
                                                 top[:, :].unsqueeze(2).to_broadcast([P, J, E]),
                                                 ALU.subtract))
                elif name == "route":
                    dve.wait_ge(s_th, b.count(1, 1))
                    step(b, 3, dve.tensor_scalar(one_plus[:, :, :], th[:, :, :], 1.0, None, ALU.add))
                    step(b, 4, dve.tensor_scalar(one_minus[:, :, :], th[:, :, :], -1.0, 1.0, ALU.mult,
                                                 ALU.add))
                    step(b, 5, dve.reciprocal(inv_minus[:, :, :], one_minus[:, :, :]))
                    step(b, 6, dve.tensor_tensor(root[:, :, :], one_plus[:, :, :], inv_minus[:, :, :],
                                                 ALU.mult))
                    step(b, 7, dve.tensor_tensor(power[:, :, :], root[:, :, :], root[:, :, :],
                                                 ALU.mult))
                    step(b, 8, dve.tensor_reduce(z[:, :], power[:, :, :], AX_X, ALU.add))
                    step(b, 9, dve.reciprocal(rz[:, :], z[:, :]))
                    step(b, 10, dve.tensor_tensor(prob[:, :, :], power[:, :, :],
                                                  rz[:, :].unsqueeze(2).to_broadcast([P, J, E]),
                                                  ALU.mult))
                    dve.wait_ge(s_lead, b.count(1, 1))
                    step(b, 11, dve.scalar_tensor_tensor(
                        tied[:, :, :], lead[:, :, :].rearrange("p (j e) f -> p j (e f)", e=E), 0.0,
                        lower.unsqueeze(1).to_broadcast([P, J, E * E]), ALU.is_ge, ALU.mult))
                    step(b, 12, dve.scalar_tensor_tensor(
                        lead[:, :, :], lead[:, :, :], 0.0,
                        tied[:, :, :].rearrange("p j (e f) -> p (j e) f", f=E), ALU.is_gt, ALU.max))
                    step(b, 13, dve.tensor_reduce(rank[:, :, :].rearrange("p j e -> p (j e)"),
                                                  lead[:, :, :], AX_X, ALU.add))
                    step(b, 14, dve.scalar_tensor_tensor(masked[:, :, :], rank[:, :, :], 2.0,
                                                         prob[:, :, :], ALU.is_lt, ALU.mult))
                    step(b, 15, dve.tensor_reduce(total[:, :], masked[:, :, :], AX_X, ALU.add))
                    step(b, 16, dve.tensor_scalar(total_eps[:, :], total[:, :], EPS_GATE, None,
                                                  ALU.add))
                    step(b, 17, dve.reciprocal(r_total[:, :], total_eps[:, :]))
                    dve.tensor_tensor(gates[:, :, :].rearrange("p e j -> p j e"), masked[:, :, :],
                                      r_total[:, :].unsqueeze(2).to_broadcast([P, J, E]),
                                      ALU.mult).then_inc(s_gates, 1)

            def step(b, n, ins):
                ins.then_inc(s_top, 1)
                dve.wait_ge(s_top, b.count(ROUTE, n))

            def gate_hidden(f, n):
                c, e = divmod(n, E)
                if e == 0:
                    dve.wait_ge(s_gall[c], f.count(16, 16))
                dve.wait_ge(s_gelu, f.count(UNITS, n + 1))
                if f.off >= 1 or n >= 4:
                    dve.wait_ge(s_l2, f.count(UNITS, n - 3))
                dve.tensor_tensor(hid_g[n % 4][:, :, :], hid[n % 2][:, :, :],
                                  gates_all[c][:, e, :].unsqueeze(1).to_broadcast([P, HH, CT]),
                                  ALU.mult).then_inc(s_hg, 1)

            def add_y(f, c):
                dve.wait_ge(s_yT, f.count(CH, c + 1))
                if f.off >= 1:
                    dve.wait_ge(s_store[c], f.count(16, 0))
                dve.tensor_tensor(y[c][:, :, :], x1[f.par][:, c * JC:(c + 1) * JC, :],
                                  ps_h[SLOT["y", c] % 2][:, 0, :].rearrange("p (j d) -> p j d", d=D),
                                  ALU.add).then_inc(s_y, 1)

            def experts(f, b):
                for n in range(UNITS):
                    if n >= 1:
                        gate_hidden(f, n - 1)
                    if b is not None:
                        for name in TICK[n]:
                            stage(b, name)
                    if n == E + 2:
                        add_y(f, 0)
                gate_hidden(f, UNITS - 1)
                add_y(f, 1)

            def modulation():
                dve.wait_ge(s_mod_ps, 1)
                dve.tensor_copy(mod[:, :, :].rearrange("p m b -> p (m b)"), ring[0][:, 0:6 * B])\
                    .then_inc(s_mod, 1)
                dve.tensor_copy(ga[:, :, :].rearrange("p b d -> p (b d)"),
                                ps_h[0][:, :, :].rearrange("p g t -> p (g t)")).then_inc(s_mod, 1)
                dve.wait_ge(s_mod, 2)
                ga_up, ga_size = (a[:, :].rearrange("p (b d) -> p b d", d=D) for a in (heads, conv))
                for m in (1, 4):
                    dve.tensor_scalar(mod[:, m, :], mod[:, m, :], 1.0, None, ALU.add)
                for g, up, size in ((mod[:, 5, :], mod_a[:, 5, :], mod_b[:, 5, :]),
                                    (ga[:, :, :], ga_up, ga_size)):
                    dve.tensor_scalar(up, g, 0.0, 2.0, ALU.is_ge, ALU.mult)
                    dve.scalar_tensor_tensor(size, g, -1.0, g, ALU.mult, ALU.max).then_inc(s_chain, 1)
                dve.wait_ge(s_chain, 2)
                for size in (mod_b[:, 5, :], ga_size):
                    dve.tensor_scalar(size, size, 0.25, None, ALU.max).then_inc(s_chain, 1)
                dve.wait_ge(s_chain, 4)
                for g, up, size in ((mod[:, 5, :], mod_a[:, 5, :], mod_b[:, 5, :]),
                                    (ga[:, :, :], ga_up, ga_size)):
                    last = dve.scalar_tensor_tensor(g, up, -1.0, size, ALU.add, ALU.mult)
                last.then_inc(s_mod, 1)
                dve.wait_ge(s_mod, 3)

            def split_weights(f, h, lo):
                dve.tensor_copy(h, f).then_inc(s_set, 1)
                done[0] += 1
                dve.wait_ge(s_set, done[0])
                dve.tensor_tensor(lo, f, h.bitcast(F32), ALU.subtract).then_inc(s_set, 1)
                done[0] += 1

            done = [4]
            dve.memset(eps_ln[:, :], EPS_LN)
            dve.memset(minus_half[:, :], -0.5).then_inc(s_set, 1)
            dve.memset(wr_f[:, E:P], 0.0).then_inc(s_set, 1)
            dve.memset(v[:, :, D:D + 1], 1.0).then_inc(s_set, 1)
            dve.memset(v_t[:, 0:PAD], 0.0)
            dve.memset(v_t[:, PAD + S:PAD + S + PAD], 0.0).then_inc(s_set, 1)
            dve.wait_ge(s_set, 4)
            dve.wait_ge(s_w["attn"], 16)
            split_weights(wqkvg_f, wqkvg_h[:, :], wqkvg_l[:, :])
            dve.wait_ge(s_w["small"], 8 * 16)
            split_weights(wr_f[:, :], wr_h[:, :], wr_l[:, :])
            dve.wait_ge(s_w["w1"], 16)
            split_weights(w1_f, w1_h[:, :, :], w1_l[:, :, :])
            schedule(dve, stage, experts)


_OUT = (B, S, D)


def kernel(**inputs):
    import numpy as np
    import concourse.bacc as bacc
    from concourse.bass_utils import run_bass_kernel_spmd as run

    a = {k: np.asarray(v) for k, v in inputs.items()}
    col = lambda v: np.ascontiguousarray(v.reshape(-1, 1))

    freq = (np.float32(1.0) / np.float32(10000.0) ** (np.arange(0, DK, 2, dtype=np.float32) / np.float32(DK)))
    angle = np.arange(S, dtype=np.float32)[:, None] * freq.astype(np.float32)[None, :]
    cos, sin = np.cos(angle), np.sin(angle)
    table = np.stack([np.concatenate([cos, cos], 1), np.concatenate([-sin, sin], 1)])
    rope = np.ascontiguousarray(table.reshape(2, J, P, DK).transpose(2, 0, 1, 3)).astype(np.float32)
    head = np.arange(P) // DK
    scale = float(DK) ** -0.5
    lower = np.tril(np.ones((E, E)), -1).reshape(1, -1).repeat(P, 0)
    consts = np.concatenate([np.eye(P), (head[:, None] == head[None, :]) * scale,
                             (head[:, None] == np.arange(HEADS)[None, :]) * scale, lower], 1)

    arrays = {
        "x": a["L0_attn_hidden_states"],
        "wqkvg": np.concatenate([a[f"L0_attn_W{n}"].T for n in "qkvg"], 1),
        "wo": a["L0_attn_Wo"].T,
        "wmod": a["L0_wmod"],
        "c_t": a["L0_c"].T,
        "lepe": np.concatenate([a["L0_attn_lepe_w"][:, 0, :], col(a["L0_attn_lepe_b"])], 1),
        "w_route": a["L0_ffn_Wg"],
        "b_route": col(a["L0_ffn_bg"]),
        "w1": a["L0_ffn_W1"].transpose(1, 0, 2),
        "b1": a["L0_ffn_b1"].reshape(E, HH, P).transpose(2, 0, 1),
        "w2": a["L0_ffn_W2"].reshape(E, HH, P, D).transpose(2, 0, 1, 3),
        "b2": a["L0_ffn_b2"],
        "rope": rope,
        "consts": consts.astype(np.float32),
    }
    arrays = {k: np.ascontiguousarray(v) for k, v in arrays.items()}
    nc = bacc.Bacc("TRN2", target_bir_lowering=False, num_devices=1)
    aps = {k: nc.dram_tensor(f"in_{k}", v.shape, mybir.dt.from_np(v.dtype), kind="ExternalInput").ap()
           for k, v in arrays.items()}
    out = nc.dram_tensor("out", _OUT, F32, kind="ExternalOutput").ap()
    adaln_moe_kernel(nc, out=out, **aps)
    r = run(nc, [{f"in_{k}": v for k, v in arrays.items()}], core_ids=[0])
    return r.results[0]["out"]
```

```python
from contextlib import ExitStack

import concourse.bass as bass
from concourse import mybir

F32 = mybir.dt.float32
F32R = mybir.dt.float32r
ALU = mybir.AluOpType
ACT = mybir.ActivationFunctionType
AX_X = mybir.AxisListType.X

P = 128
B, S, D = 8, 1024, 128
HEADS, DK = 8, 16
TAPS = 5
PAD = TAPS // 2
E, HID = 8, 256
GROUP = 32
GROUPS = 2 * GROUP + E
HH = HID // P
J = S // P
CH = 2
CT = S // CH
JC = CT // P
UNITS = CH * E
TEMP = 5.0
EPS_GATE = 1e-9
EPS_LN = 1e-5
KV = slice(D, 2 * D)

RING = 3
USES = ([("xT", c) for c in range(CH)] + [("qkv", j) for j in range(J)]
        + [("vT", c) for c in range(CH)] + [("kv", 0)] + [("qT", c) for c in range(CH)]
        + [("num", 0), ("num", 1), ("rdenT", 0), ("rdenT", 1), ("gate", 0), ("gate", 1),
           ("out", 0), ("out", 1), ("x1T", 0), ("x1T", 1), ("logit", 0), ("gatesT", 0)])
assert len(USES) % RING == 0
USE = {u: k for k, u in enumerate(USES)}
DEN = 2 * D

TICK = {0: [], 1: ["norm1"], 2: ["norm1_apply"], 3: ["xT0"], 4: ["xT1", "qkv0"], 5: ["qkv1"],
        6: ["qkv2"], 7: ["qkv3"], 8: ["vT"], 9: ["kv", "qT", "den_num"], 10: ["rdenT"],
        11: ["gate"], 12: ["out"], 13: ["norm2_apply"], 14: ["x1T0", "x1T1"], 15: ["logit"]}
LATE = {0: ["softmax"], 3: ["rank", "choice"], 4: ["gatesT"]}
STAGES = [s for k in range(UNITS) for s in TICK[k]]
TILES = {f"qkv{k}": range(2 * k, 2 * k + 2) for k in range(J // 2)}

SHIFT = 6
LAG = 3
Y_TICK = [E * (c + 1) + SHIFT + LAG for c in range(CH)]
SLOTS = []
for n in range(UNITS):
    SLOTS.append(("unit", (n - SHIFT) % UNITS, int(n < SHIFT)))
    SLOTS += [("y", c, Y_TICK[c] // UNITS) for c in range(CH) if Y_TICK[c] % UNITS == n]
assert len(SLOTS) % 2 == 0
SLOT = {(kind, i): k for k, (kind, i, _) in enumerate(SLOTS)}


FIRST_ROUND = 0


class Step:

    def __init__(self, t, off):
        self.t, self.off = t, off
        self.par = off % 2
        self.first = t is FIRST_ROUND and off == 0
        self.beyond = t is FIRST_ROUND and off == B

    def count(self, per, n=0):
        return self.t * (2 * per) + (self.off * per + n)

    def before(self):
        return Step(self.t, self.off - 1)

    def row(self):
        return bass.ds(self.t * 2 + self.off, 1)


def lagged(f, n, k):
    if n >= k:
        return None if f.beyond else (f, n - k)
    return None if f.first else (f.before(), n - k + UNITS)


def due(f, n, tick):
    if tick % UNITS != n:
        return None
    unit = lagged(f, n, tick)
    return unit and unit[0]


def stages(f, n, b, early=(), then=True):
    late = [] if f.beyond else [(f, name) for name in LATE.get(n, [])]
    ahead = [] if b is None else [(b, name) for name in TICK[n]]
    return [(at, name) for at, name in late + ahead if (name not in early) == then]


def schedule(eng, stage, tick):
    for name in STAGES:
        stage(Step(0, 0), name)
    for n in range(UNITS):
        tick(Step(0, 0), n, Step(0, 1))
    with eng.Fori(0, (B - 2) // 2) as t:
        for off in (1, 2):
            for n in range(UNITS):
                tick(Step(t, off), n, Step(t, off + 1))
    for n in range(UNITS):
        tick(Step(0, B - 1), n, None)
    for n in range(Y_TICK[CH - 1] - UNITS + 1):
        tick(Step(0, B), n, None)


def adaln_moe_kernel(nc, x, wqkvg, wo, wmod, c_t, lepe, w_route, b_route, w1, b1, w2, b2, rope,
                     consts, out):
    with ExitStack() as ctx:
        def sb(name, shape, dt=F32):
            return ctx.enter_context(nc.sbuf_tensor(name, shape, dt))

        def ps(name, shape):
            return ctx.enter_context(nc.psum_tensor(name, shape, F32))

        def sem(name):
            return ctx.enter_context(nc.semaphore(name))

        spread = sb("spread", [P, CH * E * CT])
        gates_all = [spread[:, c * E * CT:(c + 1) * E * CT].rearrange("p (e t) -> p e t", e=E)
                     for c in range(CH)]
        w1_f = spread[:, 0:E * HID].rearrange("p (e h) -> p e h", e=E)
        w2_f = spread[:, E * HID:2 * E * HID].rearrange("p (e g d) -> p e g d", e=E, g=HH)
        wqkvg_f = spread[:, 2 * E * HID:2 * E * HID + 4 * D]
        wmod_f = spread[:, 2 * E * HID + 4 * D:2 * E * HID + 10 * D]
        qk_cos, qk_sin = sb("qk_cos", [P, 2, 2 * D]), sb("qk_sin", [P, 2, 2 * D])
        wqkvg_h, wqkvg_l = sb("wqkvg_h", [P, 4 * D], F32R), sb("wqkvg_l", [P, 4 * D], F32R)
        wo_f = sb("wo_f", [P, D])
        cond = sb("cond", [P, B])
        silu = sb("silu", [P, B])
        lepe_f = sb("lepe_f", [P, TAPS + 1])
        wr_f = sb("wr_f", [P, E])
        br_f = sb("br_f", [P, E])
        w1_h, w1_l = sb("w1_h", [P, E, HID], F32R), sb("w1_l", [P, E, HID], F32R)
        b1_f = sb("b1_f", [P, E, HH])
        w2_h, w2_l = sb("w2_h", [P, E, HH, D], F32R), sb("w2_l", [P, E, HH, D], F32R)
        b2_f = sb("b2_f", [GROUPS, D])
        b2_parts = sb("b2_parts", [GROUPS, D], F32R)
        rope_f = sb("rope_f", [P, 2, J, DK])
        consts_f = sb("consts_f", [P, consts.shape[1]])
        ident = consts_f[:, 0:P]
        head_mask = consts_f[:, P:2 * P]
        head_cols = consts_f[:, 2 * P:2 * P + HEADS]
        lower = consts_f[:, 2 * P + HEADS:2 * P + HEADS + E * E]
        minus_half, eps_ln = sb("minus_half", [P, J]), sb("eps_ln", [P, J])
        scratch = sb("scratch", [P, 1])
        mod = sb("mod", [P, 6, B])
        mod_up, mod_size = sb("mod_up", [P, B]), sb("mod_size", [P, B])
        ga = sb("ga", [P, B, D])
        ga_row, ga_up, ga_size = sb("ga_row", [B, D]), sb("ga_up", [B, D]), sb("ga_size", [B, D])
        ga_dram = nc.dram_tensor("ga_dram", (B, D), F32, kind="Internal").ap()

        xs = sb("xs", [P, J, D])
        stats = sb("stats", [P, J, 6])
        mean_var = sb("mean_var", [P, J, 2])
        var_eps = sb("var_eps", [P, J])
        rstd = sb("rstd", [P, J])
        xn = sb("xn", [P, J, D])
        modc = sb("modc", [P, 6])
        wo_g = sb("wo_g", [P, D])
        h1_h, h1_l = sb("h1_h", [P, S], F32R), sb("h1_l", [P, S], F32R)
        qk = sb("qk", [P, J, 2 * D])
        v = sb("v", [P, J, D + 1])
        v_t = sb("v_t", [P, S + 2 * PAD])
        v_sums = sb("v_sums", [P, CH])
        v_sum = sb("v_sum", [P, 1])
        conv = sb("conv", [P, S])
        kv_s = sb("kv_s", [P, D])
        ksum_s = sb("ksum_s", [P, HEADS])
        q_t = xn[:, :, :].rearrange("p j d -> p (j d)")
        den = sb("den", [P, J * HEADS])
        rden = sb("rden", [P, J * HEADS])
        rden_x = qk[:, 0:JC, :].rearrange("p j (h d) -> p (j h) d", d=DK)
        heads = sb("heads", [P, S])
        h_f = heads[:, :]
        logit = sb("logit", [P, J, E])
        top = sb("top", [P, J])
        below = sb("below", [P, J, E])
        th = sb("th", [P, J, E])
        one_plus, one_minus = sb("one_plus", [P, J, E]), sb("one_minus", [P, J, E])
        inv_minus = sb("inv_minus", [P, J, E])
        root = sb("root", [P, J, E])
        power = sb("power", [P, J, E])
        z = sb("z", [P, J])
        rz = sb("rz", [P, J])
        prob = sb("prob", [P, J, E])
        lead = sb("lead", [P, J * E, E])
        tied = sb("tied", [P, J, E * E])
        rank = sb("rank", [P, J, E])
        chosen = sb("chosen", [P, J, E])
        masked = sb("masked", [P, J, E])
        total = sb("total", [P, J])
        total_eps = sb("total_eps", [P, J])
        r_total = sb("r_total", [P, J])
        gates = sb("gates", [P, E, J])
        gates_t = sb("gates_t", [E * J, P])
        gates_th, gates_tl = sb("gates_th", [E * J, P], F32R), sb("gates_tl", [E * J, P], F32R)

        x1 = [sb(f"x1_{i}", [P, J, D]) for i in range(2)]
        gb_c = [sb(f"gb_c{i}", [P, 1]) for i in range(2)]
        h2_h = [sb(f"h2_h{i}", [P, S], F32R) for i in range(2)]
        h2_l = [sb(f"h2_l{i}", [P, S], F32R) for i in range(2)]
        gates_dram = [nc.dram_tensor(f"gates_dram{i}", (E, S), F32, kind="Internal").ap() for i in range(2)]
        parts_dram = nc.dram_tensor("parts_dram", (2, E, S), F32, kind="Internal").ap()
        gates_e = sb("gates_e", [GROUPS, S], F32R)

        hid_g = [sb(f"hid_g{i}", [P, HH, CT]) for i in range(2)]
        hid_h = [sb(f"hid_h{i}", [P, HH, CT], F32R) for i in range(4)]
        hid_l = [sb(f"hid_l{i}", [P, HH, CT], F32R) for i in range(4)]
        y_t = sb("y_t", [P, CT])
        y = [sb(f"y{c}", [P, JC, D]) for c in range(CH)]

        ring = [ps(f"ring{i}", [P, 512]) for i in range(RING)]
        ps_h = [ps(f"ps_h{i}", [P, HH, CT]) for i in range(2)]
        ps_y = ps("ps_y", [P, CT])

        s_w = {k: sem(f"s_w_{k}") for k in ("attn", "mod", "ident", "small", "b2", "w1", "w2")}
        s_set = sem("s_set")
        s_high = sem("s_high")
        s_low = sem("s_low")
        s_silu = sem("s_silu")
        s_mod_ps = sem("s_mod_ps")
        s_mod = sem("s_mod")
        s_ga_row = sem("s_ga_row")
        s_ga_dram = sem("s_ga_dram")
        s_ga = sem("s_ga")
        s_chain = sem("s_chain")
        s_x = sem("s_x")
        s_stats = sem("s_stats")
        s_mv = sem("s_mv")
        s_veps = sem("s_veps")
        s_rstd = sem("s_rstd")
        s_xn = sem("s_xn")
        s_modc = sem("s_modc")
        s_xT = sem("s_xT")
        s_h1 = sem("s_h1")
        s_h1l = sem("s_h1l")
        s_qkv = sem("s_qkv")
        s_rot = sem("s_rot")
        s_v = sem("s_v")
        s_qk = sem("s_qk")
        s_vT = sem("s_vT")
        s_vt = sem("s_vt")
        s_vsum = sem("s_vsum")
        s_conv = sem("s_conv")
        s_kv = sem("s_kv")
        s_kvs = sem("s_kvs")
        s_qT = sem("s_qT")
        s_qt = sem("s_qt")
        s_den = sem("s_den")
        s_dens = sem("s_dens")
        s_rden = sem("s_rden")
        s_rdx = sem("s_rdx")
        s_num = sem("s_num")
        s_nums = sem("s_nums")
        s_rdT = sem("s_rdT")
        s_attn = sem("s_attn")
        s_mixed = sem("s_mixed")
        s_gate = sem("s_gate")
        s_ot = sem("s_ot")
        s_out = sem("s_out")
        s_x1 = sem("s_x1")
        s_x1T = sem("s_x1T")
        s_h2 = sem("s_h2")
        s_h2l = sem("s_h2l")
        s_lg = sem("s_lg")
        s_logit = sem("s_logit")
        s_top = sem("s_top")
        s_th = sem("s_th")
        s_lead = sem("s_lead")
        s_gates = sem("s_gates")
        s_gT = sem("s_gT")
        s_gts = sem("s_gts")
        s_gtl = sem("s_gtl")
        s_gd = sem("s_gd")
        s_gpd = sem("s_gpd")
        s_ge = sem("s_ge")
        s_gall = [sem(f"s_gall{c}") for c in range(CH)]
        s_l1 = sem("s_l1")
        s_gelu = sem("s_gelu")
        s_hg = sem("s_hg")
        s_hh = sem("s_hh")
        s_hl = sem("s_hl")
        s_l2 = sem("s_l2")
        s_yt = sem("s_yt")
        s_yT = sem("s_yT")
        s_y = sem("s_y")
        s_store = [sem(f"s_store{c}") for c in range(CH)]

        N_SET = 3
        N_SPLIT = 4
        ROUTE = 17

        READ = {}
        for c in range(CH):
            READ["xT", c] = (s_h1, CH, c + 1)
            READ["vT", c] = (s_vt, CH, c + 1)
            READ["qT", c] = (s_qt, CH, c + 1)
            READ["num", c] = (s_nums, CH, c + 1)
            READ["rdenT", c] = (s_attn, CH, c + 1)
            READ["gate", c] = (s_ot, CH, c + 1)
            READ["out", c] = (s_x1, CH, c + 1)
            READ["x1T", c] = (s_h2, CH, c + 1)
        for j in range(J):
            READ["qkv", j] = (s_v, J, j + 1)
        READ["kv", 0] = (s_dens, 1, 1)
        READ["logit", 0] = (s_logit, 1, 1)
        READ["gatesT", 0] = (s_gts, 1, 1)

        def ring_of(name, c=0):
            return ring[USE[name, c] % RING]

        def bank_free(eng, step, name, c=0):
            k = USE[name, c] - RING
            if k < 0 and step.off == 0:
                return
            s_read, per, n = READ[USES[k]]
            eng.wait_ge(s_read, step.count(per, n if k >= 0 else n - per))

        def hidden_bank(kind, i):
            return ps_h[SLOT[kind, i] % 2]

        def hidden_free(eng, step, kind, i):
            k = SLOT[kind, i]
            while True:
                k -= 2
                last_kind, last, wrapped = SLOTS[k]
                back = wrapped + (k < 0)
                if back or not step.beyond:
                    break
            if back and step.first:
                return
            last_step = Step(step.t, step.off - back)
            if last_kind == "y":
                eng.wait_ge(s_y, last_step.count(CH, last + 1))
            else:
                eng.wait_ge(s_hg, last_step.count(UNITS, last + 1))

        block = ctx.enter_context(nc.Block())

        @block.sync
        def _(sp):
            def load_x(b):
                if not b.first:
                    sp.wait_ge(s_x1, b.count(CH, 0))
                sp.dma_start(xs[:, :, :], x[b.row()].rearrange("a (j p) d -> p (a j) d", p=P))\
                    .then_inc(s_x, 16)

            def spread_gates(f, c):
                sp.dma_start(gates_all[c][:, :, :],
                             gates_dram[f.par][:, c * CT:(c + 1) * CT].partition_broadcast(P))\
                    .then_inc(s_gall[c], 16)

            def gates_out(f):
                if not f.first:
                    sp.wait_ge(s_l2, f.count(UNITS, E + 1 - UNITS))
                sp.wait_ge(s_gts, f.count(1, 1))
                sp.dma_start(gates_dram[f.par].rearrange("e (j t) -> (e j) t", t=P), gates_t[:, :])\
                    .then_inc(s_gd, 16)
                sp.wait_ge(s_gd, f.count(16, 16))
                spread_gates(f, 0)
                sp.wait_ge(s_gtl, f.count(1, 1))
                for k, part in enumerate((gates_th, gates_tl)):
                    sp.dma_start(parts_dram[k].rearrange("e (j t) -> (e j) t", t=P),
                                 part[:, :].bitcast(F32))\
                        .then_inc(s_gpd, 16)
                sp.wait_ge(s_gpd, f.count(32, 32))
                for g, k in enumerate((0, 0, 1)):
                    sp.dma_start(gates_e[g * GROUP:g * GROUP + E, :].bitcast(F32), parts_dram[k])\
                        .then_inc(s_ge, 16)
                if not f.first:
                    sp.wait_ge(s_hg, f.count(UNITS))
                spread_gates(f, 1)

            def store(f, c):
                sp.wait_ge(s_y, f.count(CH, c + 1))
                sp.dma_start(out[f.row()][:, c * CT:(c + 1) * CT].rearrange("a (j p) d -> p (a j) d", p=P),
                             y[c][:, :, :]).then_inc(s_store[c], 16)

            def tick(f, n, b):
                if n == 0 and b is not None:
                    load_x(b)
                if "gatesT" in LATE.get(n, []) and not f.beyond:
                    gates_out(f)
                for c in range(CH):
                    if at := due(f, n, Y_TICK[c]):
                        store(at, c)

            load_x(Step(0, 0))
            sp.dma_start(wmod_f, wmod).then_inc(s_w["mod"], 16)
            sp.dma_start(rope_f[:, :, :, :], rope).then_inc(s_w["small"], 16)
            sp.dma_start(wo_f[:, :], wo).then_inc(s_w["small"], 16)
            sp.dma_start(lepe_f[:, :], lepe).then_inc(s_w["small"], 16)
            sp.dma_start(w1_f, w1).then_inc(s_w["w1"], 16)
            sp.dma_start(w2_f, w2).then_inc(s_w["w2"], 16)
            sp.dma_start(b1_f[:, :, :], b1).then_inc(s_w["small"], 16)
            sp.dma_start(wr_f[:, :], w_route).then_inc(s_w["small"], 16)
            sp.dma_start(br_f[:, :], b_route.partition_broadcast(P)).then_inc(s_w["small"], 16)
            sp.wait_ge(s_set, N_SET)
            for g in range(3):
                sp.dma_start(b2_f[g * GROUP:g * GROUP + E, :], b2).then_inc(s_w["b2"], 16)
            sp.wait_ge(s_ga_row, 1)
            sp.dma_start(ga_dram, ga_row[:, :]).then_inc(s_ga_dram, 16)
            sp.wait_ge(s_ga_dram, 16)
            sp.dma_start(ga[:, :, :], ga_dram.partition_broadcast(P)).then_inc(s_ga, 16)
            schedule(sp, lambda b, name: None, tick)
            sp.wait_ge(s_store[0], 16 * B)
            sp.wait_ge(s_store[1], 16 * (B + 1))

        @block.tensor
        def _(pe):
            def transposes(dst, src, sem_):
                for j in range(JC):
                    last = pe.transpose(dst[:, j * P:(j + 1) * P], src(j), ident)
                last.then_inc(sem_, 1)

            def split(dst, wh, wl, ah, al):
                pe.matmul(dst, wh, ah, start=True, stop=False)
                pe.matmul(dst, wl, ah, start=False, stop=False)
                return pe.matmul(dst, wh, al, start=False, stop=True)

            def stage(b, name):
                if name in ("xT0", "xT1"):
                    c = int(name[-1])
                    if b.first:
                        pe.wait_ge(s_mod, 2)
                    pe.wait_ge(s_xn, b.count(4, c + 1))
                    bank_free(pe, b, "xT", c)
                    transposes(ring_of("xT", c), lambda j: xn[:, c * JC + j, :], s_xT)
                elif name in TILES:
                    for j in TILES[name]:
                        if b.first and j == 0:
                            pe.wait_ge(s_low, 1)
                        if j % JC == 0:
                            pe.wait_ge(s_h1l, b.count(2, j // JC + 1))
                        bank_free(pe, b, "qkv", j)
                        t = slice(j * P, (j + 1) * P)
                        w = slice(0, 3 * D)
                        split(ring_of("qkv", j)[:, w], h1_h[:, t], h1_l[:, t], wqkvg_h[:, w],
                              wqkvg_l[:, w]).then_inc(s_qkv, 1)
                elif name == "vT":
                    pe.wait_ge(s_v, b.count(J, J))
                    for c in range(CH):
                        transposes(ring_of("vT", c), lambda j: v[:, c * JC + j, 0:D], s_vT)
                elif name == "kv":
                    pe.wait_ge(s_qk, b.count(J, J))
                    bank_free(pe, b, "kv")
                    for j in range(J):
                        last = pe.matmul(ring_of("kv")[:, 0:D + 1], qk[:, j, KV], v[:, j, :],
                                         start=(j == 0), stop=(j == J - 1))
                    last.then_inc(s_kv, 1)
                elif name == "qT":
                    for c in range(CH):
                        bank_free(pe, b, "qT", c)
                        transposes(ring_of("qT", c), lambda j: qk[:, c * JC + j, 0:D], s_qT)
                elif name == "den_num":
                    pe.wait_ge(s_kvs, b.count(1, 1))
                    pe.wait_ge(s_qt, b.count(2, 2))
                    for j in range(J):
                        last = pe.matmul(ring_of("kv")[:, DEN + j * HEADS:DEN + (j + 1) * HEADS],
                                         q_t[:, j * P:(j + 1) * P], ksum_s[:, :], start=True, stop=True)
                    last.then_inc(s_den, 1)
                    for c in range(CH):
                        bank_free(pe, b, "num", c)
                        pe.matmul(ring_of("num", c)[:, :], kv_s[:, :], q_t[:, c * CT:(c + 1) * CT],
                                  start=True, stop=True).then_inc(s_num, 1)
                elif name == "rdenT":
                    for c in range(CH):
                        pe.wait_ge(s_rdx, b.count(2, c + 1))
                        bank_free(pe, b, "rdenT", c)
                        transposes(ring_of("rdenT", c),
                                   lambda j: rden_x[:, (c * JC + j) * HEADS:(c * JC + j + 1) * HEADS, :]
                                   .rearrange("p h d -> p (h d)"), s_rdT)
                elif name == "gate":
                    for c in range(CH):
                        bank_free(pe, b, "gate", c)
                        t = slice(c * CT, (c + 1) * CT)
                        w = slice(3 * D, 4 * D)
                        split(ring_of("gate", c)[:, :], wqkvg_h[:, w], wqkvg_l[:, w], h1_h[:, t],
                              h1_l[:, t]).then_inc(s_gate, 1)
                elif name == "out":
                    pe.wait_ge(s_modc, b.count(3, 2))
                    for c in range(CH):
                        pe.wait_ge(s_ot, b.count(2, c + 1))
                        if c == 0:
                            bank_free(pe, b, "out", c)
                        for j in range(JC):
                            t = c * JC + j
                            last = pe.matmul(ring_of("out", c)[:, j * P:(j + 1) * P],
                                             heads[:, t * P:(t + 1) * P], wo_g[:, :],
                                             start=True, stop=True)
                        last.then_inc(s_out, 1)
                elif name in ("x1T0", "x1T1"):
                    c = int(name[-1])
                    pe.wait_ge(s_xn, b.count(4, c + 3))
                    bank_free(pe, b, "x1T", c)
                    transposes(ring_of("x1T", c), lambda j: xn[:, c * JC + j, :], s_x1T)
                elif name == "logit":
                    if b.first:
                        pe.wait_ge(s_low, N_SPLIT)
                        pe.wait_ge(s_w["small"], 6 * 16)
                    pe.wait_ge(s_h2, b.count(2, 2))
                    bank_free(pe, b, "logit")
                    for j in range(J):
                        last = pe.matmul(ring_of("logit")[:, j * E:(j + 1) * E],
                                         h_f[:, j * P:(j + 1) * P], wr_f[:, :], start=True, stop=True)
                    last.then_inc(s_lg, 1)
                elif name == "gatesT":
                    pe.wait_ge(s_gates, b.count(1, 1))
                    bank_free(pe, b, "gatesT")
                    pe.matmul(ring_of("gatesT")[0:E * J, 0:P], gates[:, :, :].rearrange("p e j -> p (e j)"),
                              ident, start=True, stop=True).then_inc(s_gT, 1)

            def layer1(f, n, step):
                c, e = divmod(n, E)
                if n == 0:
                    pe.wait_ge(s_h2l, f.count(CH, CH))
                hidden_free(pe, step, "unit", n)
                t = slice(c * CT, (c + 1) * CT)
                for g in range(HH):
                    w = slice(g * P, (g + 1) * P)
                    last = split(hidden_bank("unit", n)[:, g, :], w1_h[:, e, w], w1_l[:, e, w],
                                 h2_h[f.par][:, t], h2_l[f.par][:, t])
                last.then_inc(s_l1, 1)

            def layer2(f, n):
                c, e = divmod(n, E)
                if e == 0:
                    pe.wait_ge(s_yt, f.count(2, c))
                    pe.wait_ge(s_ge, f.count(48, 48))
                    pe.matmul(ps_y[:, :], b2_parts[:, :], gates_e[:, c * CT:(c + 1) * CT],
                              start=True, stop=False)
                pe.wait_ge(s_hl, f.count(UNITS, n + 1))
                for g in range(HH):
                    high, low = hid_h[n % 4][:, g, :], hid_l[n % 4][:, g, :]
                    pe.matmul(ps_y[:, :], w2_h[:, e, g, :], high, start=False, stop=False)
                    pe.matmul(ps_y[:, :], w2_l[:, e, g, :], high, start=False, stop=False)
                    last = pe.matmul(ps_y[:, :], w2_h[:, e, g, :], low, start=False,
                                     stop=(e == E - 1 and g == HH - 1))
                last.then_inc(s_l2, 1)

            def turn_y(f, c, step):
                pe.wait_ge(s_yt, f.count(CH, c + 1))
                hidden_free(pe, step, "y", c)
                transposes(hidden_bank("y", c)[:, 0, :], lambda j: y_t[:, j * P:(j + 1) * P], s_yT)

            def tick(f, n, b):
                early = ("kv", "qT")
                for at, name in stages(f, n, b, early, False):
                    stage(at, name)
                if unit := lagged(f, n, SHIFT):
                    layer1(*unit, f)
                for at, name in stages(f, n, b, early):
                    stage(at, name)
                for c in range(CH):
                    if at := due(f, n, Y_TICK[c]):
                        turn_y(at, c, f)
                if unit := lagged(f, n, SHIFT + LAG):
                    layer2(*unit)

            pe.wait_ge(s_w["mod"], 32)
            pe.wait_ge(s_silu, 1)
            for m in range(6):
                pe.matmul(ring[0][:, m * B:(m + 1) * B], wmod_f[:, m * D:(m + 1) * D], silu[:, :],
                          start=True, stop=True)
            pe.matmul(ps_h[0][0:B, 0, 0:D], silu[:, :], wmod_f[:, 2 * D:3 * D],
                      start=True, stop=True).then_inc(s_mod_ps, 1)
            pe.wait_ge(s_w["ident"], 16)
            schedule(pe, stage, tick)

        @block.scalar
        def _(act):
            def stage(b, name):
                if name in ("xT0", "xT1"):
                    c = int(name[-1])
                    act.wait_ge(s_modc, b.count(3, 1))
                    act.wait_ge(s_xT, b.count(CH, c + 1))
                    t = slice(c * CT, (c + 1) * CT)
                    act.activation(h1_h[:, t], ring_of("xT", c)[:, :], ACT.Identity,
                                   bias=modc[:, 0:1], scale=modc[:, 1:2])
                    act.activation(h_f[:, t], ring_of("xT", c)[:, :], ACT.Identity,
                                   bias=modc[:, 0:1], scale=modc[:, 1:2]).then_inc(s_h1, 1)
                elif name in TILES:
                    for j in TILES[name]:
                        act.wait_ge(s_rot, b.count(J, j + 1))
                        act.activation(v[:, j, 0:D], ring_of("qkv", j)[:, 2 * D:3 * D], ACT.Copy)\
                            .then_inc(s_v, 1)
                elif name == "vT":
                    for c in range(CH):
                        act.wait_ge(s_vT, b.count(CH, c + 1))
                        act.activation(v_t[:, PAD + c * CT:PAD + (c + 1) * CT], ring_of("vT", c)[:, :],
                                       ACT.Identity, accum_out=v_sums[:, c:c + 1]).then_inc(s_vt, 1)
                elif name == "qT":
                    if b.first:
                        high_parts([1, 2, 3])
                    for c in range(CH):
                        act.wait_ge(s_qT, b.count(CH, c + 1))
                        act.activation(q_t[:, c * CT:(c + 1) * CT], ring_of("qT", c)[:, :],
                                       ACT.Copy).then_inc(s_qt, 1)
                elif name == "den_num":
                    act.wait_ge(s_vsum, b.count(1, 1))
                    for c in range(CH):
                        act.wait_ge(s_num, b.count(CH, c + 1))
                        act.activation(heads[:, c * CT:(c + 1) * CT], ring_of("num", c)[:, :],
                                       ACT.Identity, bias=v_sum[:, 0:1]).then_inc(s_nums, 1)
                    act.wait_ge(s_rden, b.count(1, 1))
                    for c in range(CH):
                        h = slice(c * JC * HEADS, (c + 1) * JC * HEADS)
                        act.activation(rden_x[:, h, :],
                                       rden[:, h].unsqueeze(2).to_broadcast([P, JC * HEADS, DK]),
                                       ACT.Copy).then_inc(s_rdx, 1)
                elif name in ("x1T0", "x1T1"):
                    c = int(name[-1])
                    act.wait_ge(s_x1T, b.count(CH, c + 1))
                    t = slice(c * CT, (c + 1) * CT)
                    act.activation(h2_h[b.par][:, t], ring_of("x1T", c)[:, :], ACT.Identity,
                                   bias=modc[:, 3:4], scale=modc[:, 4:5])
                    act.activation(h_f[:, t], ring_of("x1T", c)[:, :], ACT.Identity,
                                   bias=modc[:, 3:4], scale=modc[:, 4:5]).then_inc(s_h2, 1)
                elif name == "softmax":
                    act.wait_ge(s_top, b.count(ROUTE, 2))
                    act.activation(th[:, :, :], below[:, :, :], ACT.Tanh, scale=0.25 / TEMP)\
                        .then_inc(s_th, 1)
                elif name == "gatesT":
                    act.wait_ge(s_gT, b.count(1, 1))
                    if not b.first:
                        act.wait_ge(s_gd, b.count(16, 0))
                    act.activation(gates_t[:, :], ring_of("gatesT")[0:E * J, 0:P], ACT.Copy)
                    if not b.first:
                        act.wait_ge(s_gpd, b.count(32, 0))
                    act.activation(gates_th[:, :], ring_of("gatesT")[0:E * J, 0:P], ACT.Copy)\
                        .then_inc(s_gts, 1)

            def gelu(f, n):
                e = n % E
                act.wait_ge(s_l1, f.count(UNITS, n + 1))
                for g in range(HH):
                    bank = hidden_bank("unit", n)[:, g, :]
                    last = act.activation(bank, bank, ACT.Gelu, bias=b1_f[:, e, g:g + 1])
                last.then_inc(s_gelu, 1)

            def high_part(f, n):
                act.wait_ge(s_hg, f.count(UNITS, n + 1))
                if not (f.first and n < 4):
                    act.wait_ge(s_l2, f.count(UNITS, n - 3))
                act.activation(hid_h[n % 4][:, :, :], hid_g[n % 2][:, :, :], ACT.Copy)\
                    .then_inc(s_hh, 1)

            def take_y(f, c):
                act.wait_ge(s_l2, f.count(UNITS, E * (c + 1)))
                act.activation(y_t[:, :], ps_y[:, :], ACT.Identity, scale=gb_c[f.par][:, 0:1])\
                    .then_inc(s_yt, 1)

            def high_parts(which):
                for k in which:
                    f, h = ((wqkvg_f, wqkvg_h[:, :]), (w1_f, w1_h[:, :, :]), (w2_f, w2_h[:, :, :, :]),
                            (b2_f[:, :], b2_parts[:, :]))[k]
                    act.wait_ge(s_w[("attn", "w1", "w2", "b2")[k]], (16, 16, 16, 48)[k])
                    act.activation(h, f, ACT.Copy).then_inc(s_high, 1)

            def tick(f, n, b):
                early = ("qT", "softmax")
                for at, name in stages(f, n, b, early, False):
                    stage(at, name)
                if unit := lagged(f, n, SHIFT):
                    gelu(*unit)
                for at, name in stages(f, n, b, early):
                    stage(at, name)
                if unit := lagged(f, n, SHIFT + 1):
                    high_part(*unit)
                for c in range(CH):
                    if at := due(f, n, Y_TICK[c] - 1):
                        take_y(at, c)

            act.dma_start(cond[:, :], c_t).then_inc(s_w["mod"], 16)
            act.dma_start(wqkvg_f, wqkvg).then_inc(s_w["attn"], 16)
            act.dma_start(consts_f[:, :], consts).then_inc(s_w["ident"], 16)
            act.wait_ge(s_w["mod"], 32)
            act.activation(silu[:, :], cond[:, :], ACT.Silu).then_inc(s_silu, 1)
            high_parts([0])
            act.wait_ge(s_w["small"], 6 * 16)
            schedule(act, stage, tick)

        @block.gpsimd
        def _(pool):
            def deviation(b, n):
                pool.wait_ge(s_mv, b.count(2, n + 1))
                pool.tensor_tensor(var_eps[:, :], mean_var[:, :, 1], eps_ln[:, :], ALU.add)\
                    .then_inc(s_veps, 1)
                pool.wait_ge(s_veps, b.count(2, n + 1))
                pool.tensor_tensor(rstd[:, :], var_eps[:, :], minus_half[:, :], ALU.pow)\
                    .then_inc(s_rstd, 1)

            def stage(b, name):
                if name == "norm1":
                    deviation(b, 0)
                    if b.first:
                        low_parts([0])
                elif name in TILES:
                    for j in TILES[name]:
                        pool.wait_ge(s_rot, b.count(J, j + 1))
                        pool.tensor_tensor(qk[:, j, :], qk_cos[:, j % 2, :], qk_sin[:, j % 2, :], ALU.add)\
                            .then_inc(s_qk, 1)
                elif name == "rdenT":
                    pool.wait_ge(s_conv, b.count(TAPS, TAPS))
                    for c in range(CH):
                        pool.wait_ge(s_attn, b.count(CH, c + 1))
                        t = slice(c * CT, (c + 1) * CT)
                        pool.tensor_tensor(heads[:, t], heads[:, t], conv[:, t], ALU.add)\
                            .then_inc(s_mixed, 1)
                elif name == "den_num":
                    if b.first:
                        low_parts([1])
                elif name == "gate":
                    if b.first:
                        low_parts([2])
                elif name == "out":
                    deviation(b, 1)
                elif name == "gatesT":
                    pool.wait_ge(s_gts, b.count(1, 1))
                    if not b.first:
                        pool.wait_ge(s_gpd, b.count(32, 0))
                    pool.tensor_tensor(gates_tl[:, :], gates_t[:, :], gates_th[:, :].bitcast(F32),
                                       ALU.subtract).then_inc(s_gtl, 1)
                elif name == "logit":
                    pool.wait_ge(s_logit, b.count(1, 1))
                    pool.tensor_tensor(lead[:, :, :].rearrange("p (j e) f -> p j e f", e=E),
                                       logit[:, :, :].unsqueeze(2).to_broadcast([P, J, E, E]),
                                       logit[:, :, :].unsqueeze(3).to_broadcast([P, J, E, E]),
                                       ALU.subtract).then_inc(s_lead, 1)

            def low_part(f, n):
                pool.wait_ge(s_hh, f.count(UNITS, n + 1))
                if not (f.first and n < 4):
                    pool.wait_ge(s_l2, f.count(UNITS, n - 3))
                pool.tensor_tensor(hid_l[n % 4][:, :, :], hid_g[n % 2][:, :, :],
                                   hid_h[n % 4][:, :, :].bitcast(F32), ALU.subtract).then_inc(s_hl, 1)

            def low_parts(which):
                for k in which:
                    f, h, lo = ((wqkvg_f, wqkvg_h[:, :], wqkvg_l[:, :]),
                                (w1_f, w1_h[:, :, :], w1_l[:, :, :]),
                                (w2_f, w2_h[:, :, :, :], w2_l[:, :, :, :]))[k]
                    pool.wait_ge(s_high, k + 1)
                    pool.tensor_tensor(lo, f, h.bitcast(F32), ALU.subtract).then_inc(s_low, 1)

            def tick(f, n, b):
                for at, name in stages(f, n, b):
                    stage(at, name)
                if unit := lagged(f, n, SHIFT + 1):
                    low_part(*unit)

            pool.wait_ge(s_set, N_SET)
            schedule(pool, stage, tick)

        @block.vector
        def _(dve):
            def statistics(b, src, n):
                for j in range(J):
                    last = dve.bn_stats(stats[:, j, :], src[:, j, :])
                last.then_inc(s_stats, 1)
                dve.wait_ge(s_stats, b.count(2, n + 1))
                dve.memset(scratch[:, :], 0.0)
                for j in range(J):
                    last = dve.bn_aggr(mean_var[:, j, :], stats[:, j, :])
                last.then_inc(s_mv, 1)

            def normalise(b, src, n):
                dve.wait_ge(s_rstd, b.count(2, n + 1))
                for j in range(J):
                    last = dve.tensor_scalar(xn[:, j, :], src[:, j, :], mean_var[:, j, 0:1],
                                             rstd[:, j:j + 1], ALU.subtract, ALU.mult)
                    if j % JC == JC - 1:
                        last.then_inc(s_xn, 1)

            def halves(ap, groups=2 * HEADS):
                return ap.rearrange("p (g h d) -> p g h d", h=2, d=DK // 2)

            def table(k, j):
                return halves(rope_f[:, k, j, :]).to_broadcast([P, 2 * HEADS, 2, DK // 2])

            def stage(b, name):
                if name == "norm1":
                    dve.wait_ge(s_x, b.count(16, 16))
                    statistics(b, xs, 0)
                elif name == "norm1_apply":
                    normalise(b, xs, 0)
                    if b.first:
                        modulation()
                    dve.tensor_copy(modc[:, :].unsqueeze(2), mod[:, :, b.row()]).then_inc(s_modc, 1)
                elif name in ("xT0", "xT1"):
                    c = int(name[-1])
                    if b.first:
                        dve.wait_ge(s_w["small"], 6 * 16)
                    dve.wait_ge(s_h1, b.count(CH, c + 1))
                    t = slice(c * CT, (c + 1) * CT)
                    dve.tensor_tensor(h1_l[:, t], h_f[:, t], h1_h[:, t].bitcast(F32),
                                      ALU.subtract).then_inc(s_h1l, 1)
                elif name in TILES:
                    for j in TILES[name]:
                        dve.wait_ge(s_qkv, b.count(J, j + 1))
                        if j >= 2:
                            dve.wait_ge(s_qk, b.count(J, j - 1))
                        src = halves(ring_of("qkv", j)[:, 0:2 * D])
                        dve.tensor_tensor(halves(qk_cos[:, j % 2, :]), src, table(0, j), ALU.mult)
                        dve.tensor_tensor(halves(qk_sin[:, j % 2, :]), src[:, :, ::-1, :], table(1, j),
                                          ALU.mult).then_inc(s_rot, 1)
                elif name == "vT":
                    dve.wait_ge(s_vt, b.count(CH, CH))
                    convolve(b, 0)
                    convolve(b, 1)
                elif name == "kv":
                    dve.tensor_tensor(v_sum[:, :], v_sums[:, 0:1], v_sums[:, 1:2], ALU.add)\
                        .then_inc(s_vsum, 1)
                    dve.wait_ge(s_kv, b.count(1, 1))
                    dve.tensor_tensor(kv_s[:, :], ring_of("kv")[:, 0:D], head_mask, ALU.mult)
                    dve.tensor_scalar(ksum_s[:, :], head_cols, ring_of("kv")[:, D:D + 1], None,
                                      ALU.mult).then_inc(s_kvs, 1)
                elif name == "den_num":
                    if b.first:
                        dve.wait_ge(s_ga, 16)
                    dve.tensor_tensor(wo_g[:, :].unsqueeze(1), wo_f[:, :].unsqueeze(1),
                                      ga[:, b.row(), :], ALU.mult).then_inc(s_modc, 1)
                    convolve(b, 2)
                    dve.wait_ge(s_den, b.count(1, 1))
                    dve.tensor_scalar(den[:, :], ring_of("kv")[:, DEN:DEN + J * HEADS], float(S), None,
                                      ALU.add).then_inc(s_dens, 1)
                    dve.wait_ge(s_dens, b.count(1, 1))
                    dve.reciprocal(rden[:, :], den[:, :]).then_inc(s_rden, 1)
                    convolve(b, 3)
                elif name == "rdenT":
                    convolve(b, 4)
                    for c in range(CH):
                        dve.wait_ge(s_nums, b.count(CH, c + 1))
                        dve.wait_ge(s_rdT, b.count(CH, c + 1))
                        t = slice(c * CT, (c + 1) * CT)
                        dve.tensor_tensor(heads[:, t], heads[:, t], ring_of("rdenT", c)[:, :], ALU.mult)\
                            .then_inc(s_attn, 1)
                elif name == "gate":
                    if b.first:
                        low = slice(GROUP, GROUP + E)
                        dve.wait_ge(s_high, N_SPLIT)
                        dve.tensor_tensor(b2_parts[low, :], b2_f[low, :], b2_parts[low, :].bitcast(F32),
                                          ALU.subtract).then_inc(s_low, 1)
                    for c in range(CH):
                        dve.wait_ge(s_mixed, b.count(CH, c + 1))
                        dve.wait_ge(s_gate, b.count(CH, c + 1))
                        t = slice(c * CT, (c + 1) * CT)
                        dve.tensor_tensor(heads[:, t], heads[:, t], ring_of("gate", c)[:, :], ALU.mult)\
                            .then_inc(s_ot, 1)
                elif name == "out":
                    for c in range(CH):
                        dve.wait_ge(s_out, b.count(CH, c + 1))
                        j = slice(c * JC, (c + 1) * JC)
                        dve.tensor_tensor(x1[b.par][:, j, :], xs[:, j, :],
                                          ring_of("out", c)[:, :].rearrange("p (j d) -> p j d", d=D),
                                          ALU.add).then_inc(s_x1, 1)
                    dve.wait_ge(s_x1, b.count(CH, CH))
                    statistics(b, x1[b.par], 1)
                elif name == "norm2_apply":
                    dve.tensor_copy(gb_c[b.par][:, :].unsqueeze(2), mod[:, 5:6, b.row()])\
                        .then_inc(s_modc, 1)
                    normalise(b, x1[b.par], 1)
                elif name in ("x1T0", "x1T1"):
                    c = int(name[-1])
                    dve.wait_ge(s_h2, b.count(CH, c + 1))
                    t = slice(c * CT, (c + 1) * CT)
                    dve.tensor_tensor(h2_l[b.par][:, t], h_f[:, t], h2_h[b.par][:, t].bitcast(F32),
                                      ALU.subtract).then_inc(s_h2l, 1)
                elif name == "logit":
                    dve.wait_ge(s_lg, b.count(1, 1))
                    dve.tensor_tensor(logit[:, :, :],
                                      ring_of("logit")[:, 0:J * E].rearrange("p (j e) -> p j e", e=E),
                                      br_f[:, :].unsqueeze(1).to_broadcast([P, J, E]), ALU.add)\
                        .then_inc(s_logit, 1)
                    dve.wait_ge(s_logit, b.count(1, 1))
                    step(b, 1, dve.tensor_reduce(top[:, :], logit[:, :, :], AX_X, ALU.max))
                    step(b, 2, dve.tensor_tensor(below[:, :, :], logit[:, :, :],
                                                 top[:, :].unsqueeze(2).to_broadcast([P, J, E]),
                                                 ALU.subtract))
                elif name == "softmax":
                    dve.wait_ge(s_th, b.count(1, 1))
                    step(b, 3, dve.tensor_scalar(one_plus[:, :, :], th[:, :, :], 1.0, None, ALU.add))
                    step(b, 4, dve.tensor_scalar(one_minus[:, :, :], th[:, :, :], -1.0, 1.0, ALU.mult,
                                                 ALU.add))
                    step(b, 5, dve.reciprocal(inv_minus[:, :, :], one_minus[:, :, :]))
                    step(b, 6, dve.tensor_tensor(root[:, :, :], one_plus[:, :, :], inv_minus[:, :, :],
                                                 ALU.mult))
                    step(b, 7, dve.tensor_tensor(power[:, :, :], root[:, :, :], root[:, :, :],
                                                 ALU.mult))
                    step(b, 8, dve.tensor_reduce(z[:, :], power[:, :, :], AX_X, ALU.add))
                    step(b, 9, dve.reciprocal(rz[:, :], z[:, :]))
                    step(b, 10, dve.tensor_tensor(prob[:, :, :], power[:, :, :],
                                                  rz[:, :].unsqueeze(2).to_broadcast([P, J, E]),
                                                  ALU.mult))
                elif name == "rank":
                    dve.wait_ge(s_lead, b.count(1, 1))
                    step(b, 11, dve.scalar_tensor_tensor(
                        tied[:, :, :], lead[:, :, :].rearrange("p (j e) f -> p j (e f)", e=E), 0.0,
                        lower.unsqueeze(1).to_broadcast([P, J, E * E]), ALU.is_ge, ALU.mult))
                    step(b, 12, dve.scalar_tensor_tensor(
                        lead[:, :, :], lead[:, :, :], 0.0,
                        tied[:, :, :].rearrange("p j (e f) -> p (j e) f", f=E), ALU.is_gt, ALU.max))
                    step(b, 13, dve.tensor_reduce(rank[:, :, :].rearrange("p j e -> p (j e)"),
                                                  lead[:, :, :], AX_X, ALU.add))
                elif name == "choice":
                    step(b, 14, dve.scalar_tensor_tensor(masked[:, :, :], rank[:, :, :], 2.0,
                                                         prob[:, :, :], ALU.is_lt, ALU.mult))
                    step(b, 15, dve.tensor_reduce(total[:, :], masked[:, :, :], AX_X, ALU.add))
                    step(b, 16, dve.tensor_scalar(total_eps[:, :], total[:, :], EPS_GATE, None,
                                                  ALU.add))
                    step(b, 17, dve.reciprocal(r_total[:, :], total_eps[:, :]))
                    dve.tensor_tensor(gates[:, :, :].rearrange("p e j -> p j e"), masked[:, :, :],
                                      r_total[:, :].unsqueeze(2).to_broadcast([P, J, E]),
                                      ALU.mult).then_inc(s_gates, 1)

            def step(b, n, ins):
                ins.then_inc(s_top, 1)
                dve.wait_ge(s_top, b.count(ROUTE, n))

            def convolve(b, k):
                if k == 0:
                    dve.tensor_scalar(conv[:, :], v_t[:, 0:S], lepe_f[:, 0:1], lepe_f[:, TAPS:TAPS + 1],
                                      ALU.mult, ALU.add).then_inc(s_conv, 1)
                else:
                    dve.wait_ge(s_conv, b.count(TAPS, k))
                    dve.scalar_tensor_tensor(conv[:, :], v_t[:, k:k + S], lepe_f[:, k:k + 1],
                                             conv[:, :], ALU.mult, ALU.add).then_inc(s_conv, 1)

            def gate_hidden(f, n):
                c, e = divmod(n, E)
                if e == 0:
                    dve.wait_ge(s_gall[c], f.count(16, 16))
                dve.wait_ge(s_gelu, f.count(UNITS, n + 1))
                if not (f.first and n < 2):
                    dve.wait_ge(s_hl, f.count(UNITS, n - 1))
                dve.tensor_tensor(hid_g[n % 2][:, :, :], hidden_bank("unit", n)[:, :, :],
                                  gates_all[c][:, e, :].unsqueeze(1).to_broadcast([P, HH, CT]),
                                  ALU.mult).then_inc(s_hg, 1)

            def add_y(f, c):
                dve.wait_ge(s_yT, f.count(CH, c + 1))
                if c == 1:
                    dve.wait_ge(s_store[c], f.count(16, 16))
                elif not f.first:
                    dve.wait_ge(s_store[c], f.count(16, 0))
                dve.tensor_tensor(y[c][:, :, :], x1[f.par][:, c * JC:(c + 1) * JC, :],
                                  hidden_bank("y", c)[:, 0, :].rearrange("p (j d) -> p j d", d=D),
                                  ALU.add).then_inc(s_y, 1)

            def tick(f, n, b):
                early = ("kv",)
                for at, name in stages(f, n, b, early, False):
                    stage(at, name)
                if unit := lagged(f, n, SHIFT + 1):
                    gate_hidden(*unit)
                for at, name in stages(f, n, b, early):
                    stage(at, name)
                for c in range(CH):
                    if at := due(f, n, Y_TICK[c]):
                        add_y(at, c)

            def modulation():
                dve.wait_ge(s_mod_ps, 1)
                dve.tensor_copy(mod[:, :, :].rearrange("p m b -> p (m b)"), ring[0][:, 0:6 * B])\
                    .then_inc(s_mod, 1)
                dve.tensor_copy(ga_row[:, :], ps_h[0][0:B, 0, 0:D]).then_inc(s_mod, 1)
                dve.wait_ge(s_mod, 2)
                for m in (1, 4):
                    dve.tensor_scalar(mod[:, m, :], mod[:, m, :], 1.0, None, ALU.add)
                both = ((mod[:, 5, :], mod_up[:, :], mod_size[:, :]),
                        (ga_row[:, :], ga_up[:, :], ga_size[:, :]))
                for g, up, size in both:
                    dve.tensor_scalar(up, g, 0.0, 2.0, ALU.is_ge, ALU.mult)
                    dve.scalar_tensor_tensor(size, g, -1.0, g, ALU.mult, ALU.max).then_inc(s_chain, 1)
                dve.wait_ge(s_chain, 2)
                for _, _, size in both:
                    dve.tensor_scalar(size, size, 0.25, None, ALU.max).then_inc(s_chain, 1)
                dve.wait_ge(s_chain, 4)
                for (g, up, size), done in zip(both, (s_mod, s_ga_row)):
                    dve.scalar_tensor_tensor(g, up, -1.0, size, ALU.add, ALU.mult).then_inc(done, 1)
                dve.wait_ge(s_mod, 3)

            dve.memset(eps_ln[:, :], EPS_LN)
            dve.memset(minus_half[:, :], -0.5).then_inc(s_set, 1)
            dve.memset(b2_f[:, :], 0.0)
            dve.memset(gates_e[:, :].bitcast(F32), 0.0)
            dve.memset(v[:, :, D:D + 1], 1.0).then_inc(s_set, 1)
            dve.memset(v_t[:, 0:PAD], 0.0)
            dve.memset(v_t[:, PAD + S:PAD + S + PAD], 0.0).then_inc(s_set, 1)
            dve.memset(scratch[:, :], 0.0).then_inc(s_store[1], 16)
            schedule(dve, stage, tick)


_OUT = (B, S, D)


def kernel(**inputs):
    import numpy as np
    import concourse.bacc as bacc
    from concourse.bass_utils import run_bass_kernel_spmd as run

    a = {k: np.asarray(v) for k, v in inputs.items()}
    col = lambda v: np.ascontiguousarray(v.reshape(-1, 1))

    freq = (np.float32(1.0) / np.float32(10000.0) ** (np.arange(0, DK, 2, dtype=np.float32) / np.float32(DK)))
    angle = np.arange(S, dtype=np.float32)[:, None] * freq.astype(np.float32)[None, :]
    cos, sin = np.cos(angle), np.sin(angle)
    table = np.stack([np.concatenate([cos, cos], 1), np.concatenate([-sin, sin], 1)])
    rope = np.ascontiguousarray(table.reshape(2, J, P, DK).transpose(2, 0, 1, 3)).astype(np.float32)
    head = np.arange(P) // DK
    scale = float(DK) ** -0.5
    lower = np.tril(np.ones((E, E)), -1).reshape(1, -1).repeat(P, 0)
    consts = np.concatenate([np.eye(P), (head[:, None] == head[None, :]) * scale,
                             (head[:, None] == np.arange(HEADS)[None, :]) * scale, lower], 1)

    arrays = {
        "x": a["L0_attn_hidden_states"],
        "wqkvg": np.concatenate([a[f"L0_attn_W{n}"].T for n in "qkvg"], 1),
        "wo": a["L0_attn_Wo"].T,
        "wmod": a["L0_wmod"],
        "c_t": a["L0_c"].T,
        "lepe": np.concatenate([a["L0_attn_lepe_w"][:, 0, :], col(a["L0_attn_lepe_b"])], 1),
        "w_route": a["L0_ffn_Wg"],
        "b_route": a["L0_ffn_bg"],
        "w1": a["L0_ffn_W1"].transpose(1, 0, 2),
        "b1": a["L0_ffn_b1"].reshape(E, HH, P).transpose(2, 0, 1),
        "w2": a["L0_ffn_W2"].reshape(E, HH, P, D).transpose(2, 0, 1, 3),
        "b2": a["L0_ffn_b2"],
        "rope": rope,
        "consts": consts.astype(np.float32),
    }
    arrays = {k: np.ascontiguousarray(v) for k, v in arrays.items()}
    nc = bacc.Bacc("TRN2", target_bir_lowering=False, num_devices=1)
    aps = {k: nc.dram_tensor(f"in_{k}", v.shape, mybir.dt.from_np(v.dtype), kind="ExternalInput").ap()
           for k, v in arrays.items()}
    out = nc.dram_tensor("out", _OUT, F32, kind="ExternalOutput").ap()
    adaln_moe_kernel(nc, out=out, **aps)
    r = run(nc, [{f"in_{k}": v for k, v in arrays.items()}], core_ids=[0])
    return r.results[0]["out"]
```

```python
from contextlib import ExitStack

import concourse.bass as bass
from concourse import mybir

F32 = mybir.dt.float32
F32R = mybir.dt.float32r
ALU = mybir.AluOpType
ACT = mybir.ActivationFunctionType
AX_X = mybir.AxisListType.X

P = 128
B, S, D = 8, 1024, 128
HEADS, DK = 8, 16
TAPS = 5
PAD = TAPS // 2
E, HID = 8, 256
GROUP = 32
GROUPS = 2 * GROUP + E
HH = HID // P
J = S // P
CH = 2
CT = S // CH
JC = CT // P
UNITS = CH * E
TEMP = 5.0
EPS_GATE = 1e-9
EPS_LN = 1e-5
KV = slice(D, 2 * D)

TICK = {0: [], 1: ["norm1_0", "norm1_1"], 2: ["norm1_apply0", "norm1_apply1", "modulate"],
        3: ["xT0"], 4: ["xT1", "qkv0"], 5: ["qkv1"], 6: ["qkv2"], 7: ["qkv3"], 8: ["vT"],
        9: ["kv", "qT", "den_num"], 10: ["rdenT"], 11: ["gate"], 12: ["out0", "out1"],
        13: ["norm2_apply0", "norm2_apply1"], 14: ["x1T0", "x1T1"], 15: ["logit"]}
LATE = {0: ["softmax0"], 2: ["softmax1"], 3: ["rank0"], 4: ["rank1", "choice"], 5: ["gatesT"]}
STAGES = [s for k in range(UNITS) for s in TICK[k]]
TILES = {f"qkv{k}": range(2 * k, 2 * k + 2) for k in range(J // 2)}

SHIFT = 8
LAG = 3
Y_TICK = [E * (c + 1) + SHIFT + LAG for c in range(CH)]

RING = 3
BANKS_OF = {f"qkv{k}": [("qkv", j) for j in tiles] for k, tiles in enumerate(TILES.values())}
BANKS_OF |= {f"{n}{c}": [(n, c)] for n in ("xT", "out", "x1T") for c in range(CH)}
BANKS_OF |= {n: [(n, c) for c in range(CH)] for n in ("vT", "qT", "rdenT", "gate")}
BANKS_OF |= {"kv": [("kv", 0)], "den_num": [("den", 0), ("num", 0), ("num", 1)],
             "logit": [("logit", 0)], "gatesT": [("gatesT", 0)]}
USES = {}
HIDDEN = 2
for n in range(UNITS):
    for name in LATE.get(n, []):
        USES |= {use: 0 for use in BANKS_OF.get(name, [])}
    for name in TICK[n]:
        USES |= {use: 1 for use in BANKS_OF.get(name, [])}
    USES |= {("y", c): -(Y_TICK[c] // UNITS) for c in range(CH) if Y_TICK[c] % UNITS == n}
assert len(USES) % RING == 0 and UNITS % HIDDEN == 0


FIRST_ROUND = 0


class Step:

    def __init__(self, t, off):
        self.t, self.off = t, off
        self.par = off % 2
        self.first = t is FIRST_ROUND and off == 0
        self.beyond = t is FIRST_ROUND and off == B

    def count(self, per, n=0):
        return self.t * (2 * per) + (self.off * per + n)

    def before(self):
        return Step(self.t, self.off - 1)

    def row(self):
        return bass.ds(self.t * 2 + self.off, 1)


def last_use(use, step):
    order = list(USES)
    k = order.index(use)
    ticks = step.off - USES[use]
    while True:
        k -= RING
        rounds, place = divmod(k, len(order))
        owner = Step(step.t, ticks + rounds + USES[order[place]])
        if step.t is not FIRST_ROUND:
            assert owner.off >= 0
            return order[place], owner
        if 0 <= owner.off < B:
            return order[place], owner
        if rounds < -1 and owner.off < 0:
            return None


def lagged(f, n, k):
    if n >= k:
        return None if f.beyond else (f, n - k)
    return None if f.first else (f.before(), n - k + UNITS)


def due(f, n, tick):
    if tick % UNITS != n:
        return None
    unit = lagged(f, n, tick)
    return unit and unit[0]


def stages(f, n, b, early=(), then=True):
    late = [] if f.beyond else [(f, name) for name in LATE.get(n, [])]
    ahead = [] if b is None else [(b, name) for name in TICK[n]]
    return [(at, name) for at, name in late + ahead if (name not in early) == then]


def schedule(eng, stage, tick):
    for name in STAGES:
        stage(Step(0, 0), name)
    for n in range(UNITS):
        tick(Step(0, 0), n, Step(0, 1))
    with eng.Fori(0, (B - 2) // 2) as t:
        for off in (1, 2):
            for n in range(UNITS):
                tick(Step(t, off), n, Step(t, off + 1))
    for n in range(UNITS):
        tick(Step(0, B - 1), n, None)
    for n in range(Y_TICK[CH - 1] - UNITS + 1):
        tick(Step(0, B), n, None)


def adaln_moe_kernel(nc, x, wqkvg, wo, wmod, c_t, lepe, w_route, b_route, w1, b1, w2, b2, rope,
                     consts, out):
    with ExitStack() as ctx:
        def sb(name, shape, dt=F32):
            return ctx.enter_context(nc.sbuf_tensor(name, shape, dt))

        def ps(name, shape):
            return ctx.enter_context(nc.psum_tensor(name, shape, F32))

        def sem(name):
            return ctx.enter_context(nc.semaphore(name))

        spread = sb("spread", [P, CH * E * CT])
        gates_all = [spread[:, c * E * CT:(c + 1) * E * CT].rearrange("p (e t) -> p e t", e=E)
                     for c in range(CH)]
        w1_f = spread[:, 0:E * HID].rearrange("p (e h) -> p e h", e=E)
        w2_f = spread[:, E * HID:2 * E * HID].rearrange("p (e g d) -> p e g d", e=E, g=HH)
        wqkvg_f = spread[:, 2 * E * HID:2 * E * HID + 4 * D]
        wmod_f = spread[:, 2 * E * HID + 4 * D:2 * E * HID + 10 * D]
        qk_cos, qk_sin = sb("qk_cos", [P, 2, 2 * D]), sb("qk_sin", [P, 2, 2 * D])
        wqkvg_h, wqkvg_l = sb("wqkvg_h", [P, 4 * D], F32R), sb("wqkvg_l", [P, 4 * D], F32R)
        wo_f = sb("wo_f", [P, D])
        cond = sb("cond", [P, B])
        silu = sb("silu", [P, B])
        lepe_f = sb("lepe_f", [P, TAPS + 1])
        wr_f = sb("wr_f", [P, E])
        br_f = sb("br_f", [P, E])
        w1_h, w1_l = sb("w1_h", [P, E, HID], F32R), sb("w1_l", [P, E, HID], F32R)
        b1_f = sb("b1_f", [P, E, HH])
        w2_h, w2_l = sb("w2_h", [P, E, HH, D], F32R), sb("w2_l", [P, E, HH, D], F32R)
        b2_f = sb("b2_f", [GROUPS, D])
        b2_parts = sb("b2_parts", [GROUPS, D], F32R)
        rope_f = sb("rope_f", [P, 2, J, DK])
        consts_f = sb("consts_f", [P, consts.shape[1]])
        ident = consts_f[:, 0:P]
        head_mask = consts_f[:, P:2 * P]
        head_cols = consts_f[:, 2 * P:2 * P + HEADS]
        lower = consts_f[:, 2 * P + HEADS:2 * P + HEADS + E * E]
        minus_half, eps_ln = sb("minus_half", [P, J]), sb("eps_ln", [P, J])
        scratch = sb("scratch", [P, 1])
        mod = sb("mod", [P, 6, B])
        mod_up, mod_size = sb("mod_up", [P, B]), sb("mod_size", [P, B])
        ga = sb("ga", [P, B, D])
        ga_row, ga_up, ga_size = sb("ga_row", [B, D]), sb("ga_up", [B, D]), sb("ga_size", [B, D])
        ga_dram = nc.dram_tensor("ga_dram", (B, D), F32, kind="Internal").ap()

        xs = sb("xs", [P, J, D])
        stats = sb("stats", [P, J, 6])
        mean_var = sb("mean_var", [P, J, 2])
        var_eps = sb("var_eps", [P, J])
        rstd = sb("rstd", [P, J])
        xn = sb("xn", [P, J, D])
        modc = sb("modc", [P, 6])
        wo_g = sb("wo_g", [P, D])
        h1_h, h1_l = sb("h1_h", [P, S], F32R), sb("h1_l", [P, S], F32R)
        qk = sb("qk", [P, J, 2 * D])
        v = sb("v", [P, J, D + 1])
        v_t = sb("v_t", [P, S + 2 * PAD])
        v_sums = sb("v_sums", [P, CH])
        v_sum = sb("v_sum", [P, 1])
        conv = sb("conv", [P, S])
        kv_s = sb("kv_s", [P, D])
        ksum_s = sb("ksum_s", [P, HEADS])
        q_t = xn[:, :, :].rearrange("p j d -> p (j d)")
        den = sb("den", [P, J * HEADS])
        rden = sb("rden", [P, J * HEADS])
        rden_x = qk[:, 0:JC, :].rearrange("p j (h d) -> p (j h) d", d=DK)
        heads = sb("heads", [P, S])
        h_f = heads[:, :]
        logit = sb("logit", [P, J, E])
        top = sb("top", [P, J])
        below = sb("below", [P, J, E])
        th = sb("th", [P, J, E])
        one_plus, one_minus = sb("one_plus", [P, J, E]), sb("one_minus", [P, J, E])
        inv_minus = sb("inv_minus", [P, J, E])
        root = sb("root", [P, J, E])
        power = sb("power", [P, J, E])
        z = sb("z", [P, J])
        rz = sb("rz", [P, J])
        prob = sb("prob", [P, J, E])
        lead = sb("lead", [P, J * E, E])
        tied = sb("tied", [P, J, E * E])
        rank = sb("rank", [P, J, E])
        chosen = sb("chosen", [P, J, E])
        masked = sb("masked", [P, J, E])
        total = sb("total", [P, J])
        total_eps = sb("total_eps", [P, J])
        r_total = sb("r_total", [P, J])
        gates = sb("gates", [P, E, J])
        gates_t = sb("gates_t", [E * J, P])
        gates_th, gates_tl = sb("gates_th", [E * J, P], F32R), sb("gates_tl", [E * J, P], F32R)

        x1 = [sb(f"x1_{i}", [P, J, D]) for i in range(2)]
        gb_c = [sb(f"gb_c{i}", [P, 1]) for i in range(2)]
        h2_h = [sb(f"h2_h{i}", [P, S], F32R) for i in range(2)]
        h2_l = [sb(f"h2_l{i}", [P, S], F32R) for i in range(2)]
        gates_dram = [nc.dram_tensor(f"gates_dram{i}", (E, S), F32, kind="Internal").ap() for i in range(2)]
        parts_dram = nc.dram_tensor("parts_dram", (2, E, S), F32, kind="Internal").ap()
        gates_e = sb("gates_e", [GROUPS, S], F32R)

        hid_g = [sb(f"hid_g{i}", [P, HH, CT]) for i in range(2)]
        hid_h = [sb(f"hid_h{i}", [P, HH, CT], F32R) for i in range(4)]
        hid_l = [sb(f"hid_l{i}", [P, HH, CT], F32R) for i in range(4)]
        y_t = sb("y_t", [P, CT])
        y = [sb(f"y{c}", [P, JC, D]) for c in range(CH)]

        ring = [ps(f"ring{i}", [P, 512]) for i in range(RING)]
        ps_h = [ps(f"ps_h{i}", [P, HH, CT]) for i in range(2)]
        ps_y = ps("ps_y", [P, CT])

        s_w = {k: sem(f"s_w_{k}") for k in ("attn", "mod", "ident", "small", "b2", "w1", "w2")}
        s_set = sem("s_set")
        s_high = sem("s_high")
        s_low = sem("s_low")
        s_silu = sem("s_silu")
        s_mod_ps = sem("s_mod_ps")
        s_mod = sem("s_mod")
        s_ga_ps = sem("s_ga_ps")
        s_ga_row = sem("s_ga_row")
        s_ga_dram = sem("s_ga_dram")
        s_ga = sem("s_ga")
        s_chain = sem("s_chain")
        s_x = sem("s_x")
        s_stats = sem("s_stats")
        s_mv = sem("s_mv")
        s_veps = sem("s_veps")
        s_rstd = sem("s_rstd")
        s_xn = sem("s_xn")
        s_modc = sem("s_modc")
        s_xT = sem("s_xT")
        s_h1 = sem("s_h1")
        s_h1l = sem("s_h1l")
        s_qkv = sem("s_qkv")
        s_rot = sem("s_rot")
        s_v = sem("s_v")
        s_qk = sem("s_qk")
        s_vT = sem("s_vT")
        s_vt = sem("s_vt")
        s_vsum = sem("s_vsum")
        s_conv = sem("s_conv")
        s_kv = sem("s_kv")
        s_kvs = sem("s_kvs")
        s_qT = sem("s_qT")
        s_qt = sem("s_qt")
        s_den = sem("s_den")
        s_dens = sem("s_dens")
        s_rden = sem("s_rden")
        s_rdx = sem("s_rdx")
        s_num = sem("s_num")
        s_nums = sem("s_nums")
        s_rdT = sem("s_rdT")
        s_attn = sem("s_attn")
        s_mixed = sem("s_mixed")
        s_gate = sem("s_gate")
        s_ot = sem("s_ot")
        s_out = sem("s_out")
        s_x1 = sem("s_x1")
        s_x1T = sem("s_x1T")
        s_h2 = sem("s_h2")
        s_h2l = sem("s_h2l")
        s_lg = sem("s_lg")
        s_logit = sem("s_logit")
        s_top = sem("s_top")
        s_th = sem("s_th")
        s_lead = sem("s_lead")
        s_gates = sem("s_gates")
        s_gT = sem("s_gT")
        s_gts = sem("s_gts")
        s_gtl = sem("s_gtl")
        s_gd = sem("s_gd")
        s_gpd = sem("s_gpd")
        s_ge = sem("s_ge")
        s_gall = [sem(f"s_gall{c}") for c in range(CH)]
        s_l1 = sem("s_l1")
        s_gelu = sem("s_gelu")
        s_hg = sem("s_hg")
        s_hh = sem("s_hh")
        s_hl = sem("s_hl")
        s_l2 = sem("s_l2")
        s_yt = sem("s_yt")
        s_yT = sem("s_yT")
        s_y = sem("s_y")
        s_store = [sem(f"s_store{c}") for c in range(CH)]

        N_SET = 3
        N_SPLIT = 4
        ROUTE = 17

        READ = {}
        for c in range(CH):
            READ["xT", c] = (s_h1, CH, c + 1)
            READ["vT", c] = (s_vt, CH, c + 1)
            READ["qT", c] = (s_qt, CH, c + 1)
            READ["num", c] = (s_nums, CH, c + 1)
            READ["rdenT", c] = (s_attn, CH, c + 1)
            READ["gate", c] = (s_ot, CH, c + 1)
            READ["y", c] = (s_y, CH, c + 1)
            READ["out", c] = (s_x1, CH, c + 1)
            READ["x1T", c] = (s_h2, CH, c + 1)
        for j in range(J):
            READ["qkv", j] = (s_v, J, j + 1)
        READ["kv", 0] = (s_kvs, 1, 1)
        READ["den", 0] = (s_dens, 1, 1)
        READ["logit", 0] = (s_logit, 1, 1)
        READ["gatesT", 0] = (s_gts, 1, 1)

        def ring_of(name, c=0):
            return ring[list(USES).index((name, c)) % RING]

        def bank_free(eng, step, name, c=0):
            if last := last_use((name, c), step):
                s_read, per, n = READ[last[0]]
                eng.wait_ge(s_read, last[1].count(per, n))

        block = ctx.enter_context(nc.Block())

        @block.sync
        def _(sp):
            def load_x(b):
                if not b.first:
                    sp.wait_ge(s_x1, b.count(CH, 0))
                sp.dma_start(xs[:, :, :], x[b.row()].rearrange("a (j p) d -> p (a j) d", p=P))\
                    .then_inc(s_x, 16)

            def spread_gates(f, c):
                sp.dma_start(gates_all[c][:, :, :],
                             gates_dram[f.par][:, c * CT:(c + 1) * CT].partition_broadcast(P))\
                    .then_inc(s_gall[c], 16)

            def gates_out(f):
                if not f.first:
                    sp.wait_ge(s_l2, f.count(UNITS, E + 1 - UNITS))
                sp.wait_ge(s_gts, f.count(1, 1))
                sp.dma_start(gates_dram[f.par].rearrange("e (j t) -> (e j) t", t=P), gates_t[:, :])\
                    .then_inc(s_gd, 16)
                sp.wait_ge(s_gd, f.count(16, 16))
                spread_gates(f, 0)
                sp.wait_ge(s_gtl, f.count(1, 1))
                for k, part in enumerate((gates_th, gates_tl)):
                    sp.dma_start(parts_dram[k].rearrange("e (j t) -> (e j) t", t=P),
                                 part[:, :].bitcast(F32))\
                        .then_inc(s_gpd, 16)
                sp.wait_ge(s_gpd, f.count(32, 32))
                for g, k in enumerate((0, 0, 1)):
                    sp.dma_start(gates_e[g * GROUP:g * GROUP + E, :].bitcast(F32), parts_dram[k])\
                        .then_inc(s_ge, 16)
                if not f.first:
                    sp.wait_ge(s_hg, f.count(UNITS))
                spread_gates(f, 1)

            def store(f, c):
                sp.wait_ge(s_y, f.count(CH, c + 1))
                sp.dma_start(out[f.row()][:, c * CT:(c + 1) * CT].rearrange("a (j p) d -> p (a j) d", p=P),
                             y[c][:, :, :]).then_inc(s_store[c], 16)

            def tick(f, n, b):
                if n == 0 and b is not None:
                    load_x(b)
                if "gatesT" in LATE.get(n, []) and not f.beyond:
                    gates_out(f)
                for c in range(CH):
                    if at := due(f, n, Y_TICK[c]):
                        store(at, c)

            load_x(Step(0, 0))
            sp.dma_start(wmod_f, wmod).then_inc(s_w["mod"], 16)
            sp.dma_start(rope_f[:, :, :, :], rope).then_inc(s_w["small"], 16)
            sp.dma_start(wo_f[:, :], wo).then_inc(s_w["small"], 16)
            sp.dma_start(lepe_f[:, :], lepe).then_inc(s_w["small"], 16)
            sp.dma_start(b1_f[:, :, :], b1).then_inc(s_w["small"], 16)
            sp.dma_start(wr_f[:, :], w_route).then_inc(s_w["small"], 16)
            sp.dma_start(br_f[:, :], b_route.partition_broadcast(P)).then_inc(s_w["small"], 16)
            sp.dma_start(w1_f, w1).then_inc(s_w["w1"], 16)
            sp.dma_start(w2_f, w2).then_inc(s_w["w2"], 16)
            sp.wait_ge(s_set, N_SET)
            for g in range(3):
                sp.dma_start(b2_f[g * GROUP:g * GROUP + E, :], b2).then_inc(s_w["b2"], 16)
            sp.wait_ge(s_ga_row, 2)
            sp.dma_start(ga_dram, ga_row[:, :]).then_inc(s_ga_dram, 16)
            sp.wait_ge(s_ga_dram, 16)
            sp.dma_start(ga[:, :, :], ga_dram.partition_broadcast(P)).then_inc(s_ga, 16)
            schedule(sp, lambda b, name: None, tick)
            sp.wait_ge(s_store[0], 16 * B)
            sp.wait_ge(s_store[1], 16 * (B + 1))

        @block.tensor
        def _(pe):
            def transposes(dst, src, sem_):
                for j in range(JC):
                    last = pe.transpose(dst[:, j * P:(j + 1) * P], src(j), ident)
                last.then_inc(sem_, 1)

            def split(dst, wh, wl, ah, al):
                pe.matmul(dst, wh, ah, start=True, stop=False)
                pe.matmul(dst, wl, ah, start=False, stop=False)
                return pe.matmul(dst, wh, al, start=False, stop=True)

            def stage(b, name):
                if name in ("xT0", "xT1"):
                    c = int(name[-1])
                    if b.first:
                        pe.wait_ge(s_mod, 1)
                    pe.wait_ge(s_xn, b.count(4, c + 1))
                    bank_free(pe, b, "xT", c)
                    transposes(ring_of("xT", c), lambda j: xn[:, c * JC + j, :], s_xT)
                elif name in TILES:
                    for j in TILES[name]:
                        if b.first and j == 0:
                            pe.wait_ge(s_low, 1)
                        if j % JC == 0:
                            pe.wait_ge(s_h1l, b.count(2, j // JC + 1))
                        bank_free(pe, b, "qkv", j)
                        t = slice(j * P, (j + 1) * P)
                        w = slice(0, 3 * D)
                        split(ring_of("qkv", j)[:, w], h1_h[:, t], h1_l[:, t], wqkvg_h[:, w],
                              wqkvg_l[:, w]).then_inc(s_qkv, 1)
                elif name == "vT":
                    pe.wait_ge(s_v, b.count(J, J))
                    for c in range(CH):
                        transposes(ring_of("vT", c), lambda j: v[:, c * JC + j, 0:D], s_vT)
                elif name == "kv":
                    pe.wait_ge(s_qk, b.count(J, J))
                    bank_free(pe, b, "kv")
                    for j in range(J):
                        last = pe.matmul(ring_of("kv")[:, 0:D + 1], qk[:, j, KV], v[:, j, :],
                                         start=(j == 0), stop=(j == J - 1))
                    last.then_inc(s_kv, 1)
                elif name == "qT":
                    for c in range(CH):
                        bank_free(pe, b, "qT", c)
                        transposes(ring_of("qT", c), lambda j: qk[:, c * JC + j, 0:D], s_qT)
                elif name == "den_num":
                    pe.wait_ge(s_kvs, b.count(1, 1))
                    pe.wait_ge(s_qt, b.count(2, 2))
                    bank_free(pe, b, "den")
                    for j in range(J):
                        last = pe.matmul(ring_of("den")[:, j * HEADS:(j + 1) * HEADS],
                                         q_t[:, j * P:(j + 1) * P], ksum_s[:, :], start=True, stop=True)
                    last.then_inc(s_den, 1)
                    for c in range(CH):
                        bank_free(pe, b, "num", c)
                        pe.matmul(ring_of("num", c)[:, :], kv_s[:, :], q_t[:, c * CT:(c + 1) * CT],
                                  start=True, stop=True).then_inc(s_num, 1)
                elif name == "rdenT":
                    for c in range(CH):
                        pe.wait_ge(s_rdx, b.count(2, c + 1))
                        bank_free(pe, b, "rdenT", c)
                        transposes(ring_of("rdenT", c),
                                   lambda j: rden_x[:, (c * JC + j) * HEADS:(c * JC + j + 1) * HEADS, :]
                                   .rearrange("p h d -> p (h d)"), s_rdT)
                elif name == "gate":
                    for c in range(CH):
                        bank_free(pe, b, "gate", c)
                        t = slice(c * CT, (c + 1) * CT)
                        w = slice(3 * D, 4 * D)
                        split(ring_of("gate", c)[:, :], wqkvg_h[:, w], wqkvg_l[:, w], h1_h[:, t],
                              h1_l[:, t]).then_inc(s_gate, 1)
                elif name in ("out0", "out1"):
                    c = int(name[-1])
                    pe.wait_ge(s_modc, b.count(3, 2))
                    pe.wait_ge(s_ot, b.count(2, c + 1))
                    if c == 0:
                        bank_free(pe, b, "out", c)
                    for j in range(JC):
                        t = c * JC + j
                        last = pe.matmul(ring_of("out", c)[:, j * P:(j + 1) * P],
                                         heads[:, t * P:(t + 1) * P], wo_g[:, :],
                                         start=True, stop=True)
                    last.then_inc(s_out, 1)
                elif name in ("x1T0", "x1T1"):
                    c = int(name[-1])
                    pe.wait_ge(s_xn, b.count(4, c + 3))
                    bank_free(pe, b, "x1T", c)
                    transposes(ring_of("x1T", c), lambda j: xn[:, c * JC + j, :], s_x1T)
                elif name == "logit":
                    if b.first:
                        pe.wait_ge(s_w["small"], 6 * 16)
                    pe.wait_ge(s_h2, b.count(2, 2))
                    bank_free(pe, b, "logit")
                    for j in range(J):
                        last = pe.matmul(ring_of("logit")[:, j * E:(j + 1) * E],
                                         h_f[:, j * P:(j + 1) * P], wr_f[:, :], start=True, stop=True)
                    last.then_inc(s_lg, 1)
                elif name == "gatesT":
                    if b.first:
                        pe.wait_ge(s_low, N_SPLIT)
                    pe.wait_ge(s_gates, b.count(1, 1))
                    bank_free(pe, b, "gatesT")
                    pe.matmul(ring_of("gatesT")[0:E * J, 0:P], gates[:, :, :].rearrange("p e j -> p (e j)"),
                              ident, start=True, stop=True).then_inc(s_gT, 1)

            def layer1(f, n):
                c, e = divmod(n, E)
                if n == 0:
                    pe.wait_ge(s_h2l, f.count(CH, CH))
                if not (f.first and n < HIDDEN):
                    pe.wait_ge(s_hg, f.count(UNITS, n + 1 - HIDDEN))
                t = slice(c * CT, (c + 1) * CT)
                for g in range(HH):
                    w = slice(g * P, (g + 1) * P)
                    last = split(ps_h[n % HIDDEN][:, g, :], w1_h[:, e, w], w1_l[:, e, w],
                                 h2_h[f.par][:, t], h2_l[f.par][:, t])
                last.then_inc(s_l1, 1)

            def layer2(f, n):
                c, e = divmod(n, E)
                if e == 0:
                    pe.wait_ge(s_yt, f.count(2, c))
                    pe.wait_ge(s_ge, f.count(48, 48))
                    pe.matmul(ps_y[:, :], b2_parts[:, :], gates_e[:, c * CT:(c + 1) * CT],
                              start=True, stop=False)
                pe.wait_ge(s_hl, f.count(UNITS, n + 1))
                for g in range(HH):
                    high, low = hid_h[n % 4][:, g, :], hid_l[n % 4][:, g, :]
                    pe.matmul(ps_y[:, :], w2_h[:, e, g, :], high, start=False, stop=False)
                    pe.matmul(ps_y[:, :], w2_l[:, e, g, :], high, start=False, stop=False)
                    last = pe.matmul(ps_y[:, :], w2_h[:, e, g, :], low, start=False,
                                     stop=(e == E - 1 and g == HH - 1))
                last.then_inc(s_l2, 1)

            def turn_y(f, c):
                pe.wait_ge(s_yt, f.count(CH, c + 1))
                bank_free(pe, f, "y", c)
                transposes(ring_of("y", c)[:, :], lambda j: y_t[:, j * P:(j + 1) * P], s_yT)

            def tick(f, n, b):
                early = ("kv", "out0", "out1", "qT", "gate")
                for at, name in stages(f, n, b, early, False):
                    stage(at, name)
                if unit := lagged(f, n, SHIFT):
                    layer1(*unit)
                for at, name in stages(f, n, b, early):
                    stage(at, name)
                for c in range(CH):
                    if at := due(f, n, Y_TICK[c]):
                        turn_y(at, c)
                if unit := lagged(f, n, SHIFT + LAG):
                    layer2(*unit)

            pe.wait_ge(s_w["mod"], 32)
            pe.wait_ge(s_silu, 1)
            for m in range(6):
                last = pe.matmul(ring[0][:, m * B:(m + 1) * B], wmod_f[:, m * D:(m + 1) * D],
                                 silu[:, :], start=True, stop=True)
            last.then_inc(s_mod_ps, 1)
            pe.matmul(ps_h[0][0:B, 0, 0:D], silu[:, :], wmod_f[:, 2 * D:3 * D],
                      start=True, stop=True).then_inc(s_ga_ps, 1)
            pe.wait_ge(s_w["ident"], 16)
            schedule(pe, stage, tick)

        @block.scalar
        def _(act):
            def stage(b, name):
                if name in ("xT0", "xT1"):
                    c = int(name[-1])
                    act.wait_ge(s_modc, b.count(3, 1))
                    act.wait_ge(s_xT, b.count(CH, c + 1))
                    t = slice(c * CT, (c + 1) * CT)
                    act.activation(h1_h[:, t], ring_of("xT", c)[:, :], ACT.Identity,
                                   bias=modc[:, 0:1], scale=modc[:, 1:2])
                    act.activation(h_f[:, t], ring_of("xT", c)[:, :], ACT.Identity,
                                   bias=modc[:, 0:1], scale=modc[:, 1:2]).then_inc(s_h1, 1)
                elif name in TILES:
                    for j in TILES[name]:
                        act.wait_ge(s_rot, b.count(J, j + 1))
                        act.activation(v[:, j, 0:D], ring_of("qkv", j)[:, 2 * D:3 * D], ACT.Copy)\
                            .then_inc(s_v, 1)
                elif name == "vT":
                    for c in range(CH):
                        act.wait_ge(s_vT, b.count(CH, c + 1))
                        act.activation(v_t[:, PAD + c * CT:PAD + (c + 1) * CT], ring_of("vT", c)[:, :],
                                       ACT.Identity, accum_out=v_sums[:, c:c + 1]).then_inc(s_vt, 1)
                elif name == "qT":
                    for c in range(CH):
                        act.wait_ge(s_qT, b.count(CH, c + 1))
                        act.activation(q_t[:, c * CT:(c + 1) * CT], ring_of("qT", c)[:, :],
                                       ACT.Copy).then_inc(s_qt, 1)
                elif name == "den_num":
                    act.wait_ge(s_rden, b.count(1, 1))
                    for c in range(CH):
                        h = slice(c * JC * HEADS, (c + 1) * JC * HEADS)
                        act.activation(rden_x[:, h, :],
                                       rden[:, h].unsqueeze(2).to_broadcast([P, JC * HEADS, DK]),
                                       ACT.Copy).then_inc(s_rdx, 1)
                    act.wait_ge(s_vsum, b.count(1, 1))
                    for c in range(CH):
                        act.wait_ge(s_num, b.count(CH, c + 1))
                        act.activation(heads[:, c * CT:(c + 1) * CT], ring_of("num", c)[:, :],
                                       ACT.Identity, bias=v_sum[:, 0:1]).then_inc(s_nums, 1)
                elif name == "rdenT":
                    if b.first:
                        high_parts([1, 2, 3])
                        act.wait_ge(s_w["small"], 6 * 16)
                elif name in ("x1T0", "x1T1"):
                    c = int(name[-1])
                    act.wait_ge(s_x1T, b.count(CH, c + 1))
                    t = slice(c * CT, (c + 1) * CT)
                    act.activation(h2_h[b.par][:, t], ring_of("x1T", c)[:, :], ACT.Identity,
                                   bias=modc[:, 3:4], scale=modc[:, 4:5])
                    act.activation(h_f[:, t], ring_of("x1T", c)[:, :], ACT.Identity,
                                   bias=modc[:, 3:4], scale=modc[:, 4:5]).then_inc(s_h2, 1)
                elif name == "softmax0":
                    act.wait_ge(s_top, b.count(ROUTE, 2))
                    act.activation(th[:, :, :], below[:, :, :], ACT.Tanh, scale=0.25 / TEMP)\
                        .then_inc(s_th, 1)
                elif name == "gatesT":
                    act.wait_ge(s_gT, b.count(1, 1))
                    if not b.first:
                        act.wait_ge(s_gd, b.count(16, 0))
                    act.activation(gates_t[:, :], ring_of("gatesT")[0:E * J, 0:P], ACT.Copy)
                    if not b.first:
                        act.wait_ge(s_gpd, b.count(32, 0))
                    act.activation(gates_th[:, :], ring_of("gatesT")[0:E * J, 0:P], ACT.Copy)\
                        .then_inc(s_gts, 1)

            def gelu(f, n):
                e = n % E
                act.wait_ge(s_l1, f.count(UNITS, n + 1))
                for g in range(HH):
                    bank = ps_h[n % HIDDEN][:, g, :]
                    last = act.activation(bank, bank, ACT.Gelu, bias=b1_f[:, e, g:g + 1])
                last.then_inc(s_gelu, 1)

            def high_part(f, n):
                act.wait_ge(s_hg, f.count(UNITS, n + 1))
                if not (f.first and n < 4):
                    act.wait_ge(s_l2, f.count(UNITS, n - 3))
                act.activation(hid_h[n % 4][:, :, :], hid_g[n % 2][:, :, :], ACT.Copy)\
                    .then_inc(s_hh, 1)

            def take_y(f, c):
                act.wait_ge(s_l2, f.count(UNITS, E * (c + 1)))
                act.activation(y_t[:, :], ps_y[:, :], ACT.Identity, scale=gb_c[f.par][:, 0:1])\
                    .then_inc(s_yt, 1)

            def high_parts(which):
                for k in which:
                    f, h = ((wqkvg_f, wqkvg_h[:, :]), (w1_f, w1_h[:, :, :]), (w2_f, w2_h[:, :, :, :]),
                            (b2_f[:, :], b2_parts[:, :]))[k]
                    act.wait_ge(s_w[("attn", "w1", "w2", "b2")[k]], (16, 16, 16, 48)[k])
                    act.activation(h, f, ACT.Copy).then_inc(s_high, 1)

            def tick(f, n, b):
                early = ("qT", "softmax0")
                for at, name in stages(f, n, b, early, False):
                    stage(at, name)
                if unit := lagged(f, n, SHIFT):
                    gelu(*unit)
                for at, name in stages(f, n, b, early):
                    stage(at, name)
                for c in range(CH):
                    if at := due(f, n, Y_TICK[c] - 1):
                        take_y(at, c)
                if unit := lagged(f, n, SHIFT + 1):
                    high_part(*unit)

            act.dma_start(cond[:, :], c_t).then_inc(s_w["mod"], 16)
            act.dma_start(wqkvg_f, wqkvg).then_inc(s_w["attn"], 16)
            act.dma_start(consts_f[:, :], consts).then_inc(s_w["ident"], 16)
            act.wait_ge(s_w["mod"], 32)
            act.activation(silu[:, :], cond[:, :], ACT.Silu).then_inc(s_silu, 1)
            high_parts([0])
            schedule(act, stage, tick)

        @block.gpsimd
        def _(pool):
            def deviation(b, n, c):
                j = slice(c * JC, (c + 1) * JC)
                done = b.count(2 * CH, n * CH + c + 1)
                pool.wait_ge(s_mv, done)
                pool.tensor_tensor(var_eps[:, j], mean_var[:, j, 1], eps_ln[:, j], ALU.add)\
                    .then_inc(s_veps, 1)
                pool.wait_ge(s_veps, done)
                pool.tensor_tensor(rstd[:, j], var_eps[:, j], minus_half[:, j], ALU.pow)\
                    .then_inc(s_rstd, 1)

            def stage(b, name):
                if name in ("norm1_0", "norm1_1"):
                    deviation(b, 0, int(name[-1]))
                elif name == "modulate":
                    if b.first:
                        low_parts([0])
                elif name in ("xT0", "xT1"):
                    c = int(name[-1])
                    pool.wait_ge(s_h1, b.count(CH, c + 1))
                    t = slice(c * CT, (c + 1) * CT)
                    pool.tensor_tensor(h1_l[:, t], h_f[:, t], h1_h[:, t].bitcast(F32),
                                      ALU.subtract).then_inc(s_h1l, 1)
                elif name in TILES:
                    for j in TILES[name]:
                        pool.wait_ge(s_rot, b.count(J, j + 1))
                        pool.tensor_tensor(qk[:, j, :], qk_cos[:, j % 2, :], qk_sin[:, j % 2, :], ALU.add)\
                            .then_inc(s_qk, 1)
                elif name == "rdenT":
                    pool.wait_ge(s_conv, b.count(TAPS, TAPS))
                    for c in range(CH):
                        pool.wait_ge(s_attn, b.count(CH, c + 1))
                        t = slice(c * CT, (c + 1) * CT)
                        pool.tensor_tensor(heads[:, t], heads[:, t], conv[:, t], ALU.add)\
                            .then_inc(s_mixed, 1)
                elif name in ("out0", "out1"):
                    deviation(b, 1, int(name[-1]))
                elif name == "norm2_apply1":
                    if b.first:
                        low_parts([1, 2])
                elif name == "gatesT":
                    pool.wait_ge(s_gts, b.count(1, 1))
                    if not b.first:
                        pool.wait_ge(s_gpd, b.count(32, 0))
                    pool.tensor_tensor(gates_tl[:, :], gates_t[:, :], gates_th[:, :].bitcast(F32),
                                       ALU.subtract).then_inc(s_gtl, 1)
                elif name == "logit":
                    pool.wait_ge(s_logit, b.count(1, 1))
                    pool.tensor_tensor(lead[:, :, :].rearrange("p (j e) f -> p j e f", e=E),
                                       logit[:, :, :].unsqueeze(2).to_broadcast([P, J, E, E]),
                                       logit[:, :, :].unsqueeze(3).to_broadcast([P, J, E, E]),
                                       ALU.subtract).then_inc(s_lead, 1)

            def low_part(f, n):
                pool.wait_ge(s_hh, f.count(UNITS, n + 1))
                if not (f.first and n < 4):
                    pool.wait_ge(s_l2, f.count(UNITS, n - 3))
                pool.tensor_tensor(hid_l[n % 4][:, :, :], hid_g[n % 2][:, :, :],
                                   hid_h[n % 4][:, :, :].bitcast(F32), ALU.subtract).then_inc(s_hl, 1)

            def low_parts(which):
                for k in which:
                    f, h, lo = ((wqkvg_f, wqkvg_h[:, :], wqkvg_l[:, :]),
                                (w1_f, w1_h[:, :, :], w1_l[:, :, :]),
                                (w2_f, w2_h[:, :, :, :], w2_l[:, :, :, :]))[k]
                    pool.wait_ge(s_high, k + 1)
                    pool.tensor_tensor(lo, f, h.bitcast(F32), ALU.subtract).then_inc(s_low, 1)

            def tick(f, n, b):
                for at, name in stages(f, n, b):
                    stage(at, name)
                if unit := lagged(f, n, SHIFT + 1):
                    low_part(*unit)

            pool.wait_ge(s_set, N_SET)
            schedule(pool, stage, tick)

        @block.vector
        def _(dve):
            def statistics(b, src, n, c):
                for j in range(c * JC, (c + 1) * JC):
                    last = dve.bn_stats(stats[:, j, :], src[:, j, :])
                last.then_inc(s_stats, 1)
                dve.wait_ge(s_stats, b.count(2 * CH, n * CH + c + 1))
                dve.memset(scratch[:, :], 0.0)
                for j in range(c * JC, (c + 1) * JC):
                    last = dve.bn_aggr(mean_var[:, j, :], stats[:, j, :])
                last.then_inc(s_mv, 1)

            def normalise(b, src, n, c):
                dve.wait_ge(s_rstd, b.count(2 * CH, n * CH + c + 1))
                for j in range(c * JC, (c + 1) * JC):
                    last = dve.tensor_scalar(xn[:, j, :], src[:, j, :], mean_var[:, j, 0:1],
                                             rstd[:, j:j + 1], ALU.subtract, ALU.mult)
                last.then_inc(s_xn, 1)

            def halves(ap, groups=2 * HEADS):
                return ap.rearrange("p (g h d) -> p g h d", h=2, d=DK // 2)

            def table(k, j):
                return halves(rope_f[:, k, j, :]).to_broadcast([P, 2 * HEADS, 2, DK // 2])

            def stage(b, name):
                if name in ("norm1_0", "norm1_1"):
                    if name == "norm1_0":
                        dve.wait_ge(s_x, b.count(16, 16))
                    statistics(b, xs, 0, int(name[-1]))
                elif name in ("norm1_apply0", "norm1_apply1"):
                    normalise(b, xs, 0, int(name[-1]))
                elif name == "modulate":
                    if b.first:
                        modulation()
                    dve.tensor_copy(modc[:, :].unsqueeze(2), mod[:, :, b.row()]).then_inc(s_modc, 1)
                    if b.first:
                        gate_row()
                elif name == "xT0":
                    if b.first:
                        dve.wait_ge(s_w["small"], 6 * 16)
                elif name in TILES:
                    for j in TILES[name]:
                        dve.wait_ge(s_qkv, b.count(J, j + 1))
                        if j >= 2:
                            dve.wait_ge(s_qk, b.count(J, j - 1))
                        src = halves(ring_of("qkv", j)[:, 0:2 * D])
                        dve.tensor_tensor(halves(qk_cos[:, j % 2, :]), src, table(0, j), ALU.mult)
                        dve.tensor_tensor(halves(qk_sin[:, j % 2, :]), src[:, :, ::-1, :], table(1, j),
                                          ALU.mult).then_inc(s_rot, 1)
                elif name == "vT":
                    dve.wait_ge(s_vt, b.count(CH, CH))
                    convolve(b, 0)
                    convolve(b, 1)
                elif name == "kv":
                    dve.tensor_tensor(v_sum[:, :], v_sums[:, 0:1], v_sums[:, 1:2], ALU.add)\
                        .then_inc(s_vsum, 1)
                    dve.wait_ge(s_kv, b.count(1, 1))
                    dve.tensor_tensor(kv_s[:, :], ring_of("kv")[:, 0:D], head_mask, ALU.mult)
                    dve.tensor_scalar(ksum_s[:, :], head_cols, ring_of("kv")[:, D:D + 1], None,
                                      ALU.mult).then_inc(s_kvs, 1)
                elif name == "den_num":
                    if b.first:
                        dve.wait_ge(s_ga, 16)
                    dve.tensor_tensor(wo_g[:, :].unsqueeze(1), wo_f[:, :].unsqueeze(1),
                                      ga[:, b.row(), :], ALU.mult).then_inc(s_modc, 1)
                    convolve(b, 2)
                    dve.wait_ge(s_den, b.count(1, 1))
                    dve.tensor_scalar(den[:, :], ring_of("den")[:, 0:J * HEADS], float(S), None,
                                      ALU.add).then_inc(s_dens, 1)
                    dve.wait_ge(s_dens, b.count(1, 1))
                    dve.reciprocal(rden[:, :], den[:, :]).then_inc(s_rden, 1)
                    convolve(b, 3)
                elif name == "rdenT":
                    convolve(b, 4)
                    for c in range(CH):
                        dve.wait_ge(s_nums, b.count(CH, c + 1))
                        dve.wait_ge(s_rdT, b.count(CH, c + 1))
                        t = slice(c * CT, (c + 1) * CT)
                        dve.tensor_tensor(heads[:, t], heads[:, t], ring_of("rdenT", c)[:, :], ALU.mult)\
                            .then_inc(s_attn, 1)
                elif name == "gate":
                    for c in range(CH):
                        dve.wait_ge(s_mixed, b.count(CH, c + 1))
                        dve.wait_ge(s_gate, b.count(CH, c + 1))
                        t = slice(c * CT, (c + 1) * CT)
                        dve.tensor_tensor(heads[:, t], heads[:, t], ring_of("gate", c)[:, :], ALU.mult)\
                            .then_inc(s_ot, 1)
                elif name in ("out0", "out1"):
                    c = int(name[-1])
                    dve.wait_ge(s_out, b.count(CH, c + 1))
                    j = slice(c * JC, (c + 1) * JC)
                    dve.tensor_tensor(x1[b.par][:, j, :], xs[:, j, :],
                                      ring_of("out", c)[:, :].rearrange("p (j d) -> p j d", d=D),
                                      ALU.add).then_inc(s_x1, 1)
                    dve.wait_ge(s_x1, b.count(CH, c + 1))
                    statistics(b, x1[b.par], 1, c)
                elif name == "norm2_apply0":
                    if b.first:
                        low = slice(GROUP, GROUP + E)
                        dve.wait_ge(s_high, N_SPLIT)
                        dve.tensor_tensor(b2_parts[low, :], b2_f[low, :], b2_parts[low, :].bitcast(F32),
                                          ALU.subtract).then_inc(s_low, 1)
                    dve.tensor_copy(gb_c[b.par][:, :].unsqueeze(2), mod[:, 5:6, b.row()])\
                        .then_inc(s_modc, 1)
                    normalise(b, x1[b.par], 1, 0)
                elif name == "norm2_apply1":
                    normalise(b, x1[b.par], 1, 1)
                elif name in ("x1T0", "x1T1"):
                    c = int(name[-1])
                    dve.wait_ge(s_h2, b.count(CH, c + 1))
                    t = slice(c * CT, (c + 1) * CT)
                    dve.tensor_tensor(h2_l[b.par][:, t], h_f[:, t], h2_h[b.par][:, t].bitcast(F32),
                                      ALU.subtract).then_inc(s_h2l, 1)
                elif name == "logit":
                    dve.wait_ge(s_lg, b.count(1, 1))
                    dve.tensor_tensor(logit[:, :, :],
                                      ring_of("logit")[:, 0:J * E].rearrange("p (j e) -> p j e", e=E),
                                      br_f[:, :].unsqueeze(1).to_broadcast([P, J, E]), ALU.add)\
                        .then_inc(s_logit, 1)
                    dve.wait_ge(s_logit, b.count(1, 1))
                    step(b, 1, dve.tensor_reduce(top[:, :], logit[:, :, :], AX_X, ALU.max))
                    step(b, 2, dve.tensor_tensor(below[:, :, :], logit[:, :, :],
                                                 top[:, :].unsqueeze(2).to_broadcast([P, J, E]),
                                                 ALU.subtract))
                elif name == "softmax0":
                    dve.wait_ge(s_th, b.count(1, 1))
                    step(b, 3, dve.tensor_scalar(one_plus[:, :, :], th[:, :, :], 1.0, None, ALU.add))
                    step(b, 4, dve.tensor_scalar(one_minus[:, :, :], th[:, :, :], -1.0, 1.0, ALU.mult,
                                                 ALU.add))
                    step(b, 5, dve.reciprocal(inv_minus[:, :, :], one_minus[:, :, :]))
                    step(b, 6, dve.tensor_tensor(root[:, :, :], one_plus[:, :, :], inv_minus[:, :, :],
                                                 ALU.mult))
                    step(b, 7, dve.tensor_tensor(power[:, :, :], root[:, :, :], root[:, :, :],
                                                 ALU.mult))
                elif name == "softmax1":
                    step(b, 8, dve.tensor_reduce(z[:, :], power[:, :, :], AX_X, ALU.add))
                    step(b, 9, dve.reciprocal(rz[:, :], z[:, :]))
                    step(b, 10, dve.tensor_tensor(prob[:, :, :], power[:, :, :],
                                                  rz[:, :].unsqueeze(2).to_broadcast([P, J, E]),
                                                  ALU.mult))
                elif name == "rank0":
                    dve.wait_ge(s_lead, b.count(1, 1))
                    step(b, 11, dve.scalar_tensor_tensor(
                        tied[:, :, :], lead[:, :, :].rearrange("p (j e) f -> p j (e f)", e=E), 0.0,
                        lower.unsqueeze(1).to_broadcast([P, J, E * E]), ALU.is_ge, ALU.mult))
                elif name == "rank1":
                    step(b, 12, dve.scalar_tensor_tensor(
                        lead[:, :, :], lead[:, :, :], 0.0,
                        tied[:, :, :].rearrange("p j (e f) -> p (j e) f", f=E), ALU.is_gt, ALU.max))
                    step(b, 13, dve.tensor_reduce(rank[:, :, :].rearrange("p j e -> p (j e)"),
                                                  lead[:, :, :], AX_X, ALU.add))
                elif name == "choice":
                    step(b, 14, dve.scalar_tensor_tensor(masked[:, :, :], rank[:, :, :], 2.0,
                                                         prob[:, :, :], ALU.is_lt, ALU.mult))
                    step(b, 15, dve.tensor_reduce(total[:, :], masked[:, :, :], AX_X, ALU.add))
                    step(b, 16, dve.tensor_scalar(total_eps[:, :], total[:, :], EPS_GATE, None,
                                                  ALU.add))
                    step(b, 17, dve.reciprocal(r_total[:, :], total_eps[:, :]))
                    dve.tensor_tensor(gates[:, :, :].rearrange("p e j -> p j e"), masked[:, :, :],
                                      r_total[:, :].unsqueeze(2).to_broadcast([P, J, E]),
                                      ALU.mult).then_inc(s_gates, 1)

            def step(b, n, ins):
                ins.then_inc(s_top, 1)
                dve.wait_ge(s_top, b.count(ROUTE, n))

            def convolve(b, k):
                if k == 0:
                    dve.tensor_scalar(conv[:, :], v_t[:, 0:S], lepe_f[:, 0:1], lepe_f[:, TAPS:TAPS + 1],
                                      ALU.mult, ALU.add).then_inc(s_conv, 1)
                else:
                    dve.wait_ge(s_conv, b.count(TAPS, k))
                    dve.scalar_tensor_tensor(conv[:, :], v_t[:, k:k + S], lepe_f[:, k:k + 1],
                                             conv[:, :], ALU.mult, ALU.add).then_inc(s_conv, 1)

            def gate_hidden(f, n):
                c, e = divmod(n, E)
                if e == 0:
                    dve.wait_ge(s_gall[c], f.count(16, 16))
                dve.wait_ge(s_gelu, f.count(UNITS, n + 1))
                if not (f.first and n < 2):
                    dve.wait_ge(s_hl, f.count(UNITS, n - 1))
                dve.tensor_tensor(hid_g[n % 2][:, :, :], ps_h[n % HIDDEN][:, :, :],
                                  gates_all[c][:, e, :].unsqueeze(1).to_broadcast([P, HH, CT]),
                                  ALU.mult).then_inc(s_hg, 1)

            def add_y(f, c):
                dve.wait_ge(s_yT, f.count(CH, c + 1))
                if c == 1:
                    dve.wait_ge(s_store[c], f.count(16, 16))
                elif not f.first:
                    dve.wait_ge(s_store[c], f.count(16, 0))
                dve.tensor_tensor(y[c][:, :, :], x1[f.par][:, c * JC:(c + 1) * JC, :],
                                  ring_of("y", c)[:, :].rearrange("p (j d) -> p j d", d=D),
                                  ALU.add).then_inc(s_y, 1)

            def tick(f, n, b):
                early = ("kv", "norm1_0")
                for at, name in stages(f, n, b, early, False):
                    stage(at, name)
                if unit := lagged(f, n, SHIFT + 1):
                    gate_hidden(*unit)
                for at, name in stages(f, n, b, early):
                    stage(at, name)
                for c in range(CH):
                    if at := due(f, n, Y_TICK[c]):
                        add_y(at, c)

            def at_least(g, up, size, start, done):
                dve.tensor_scalar(up, g, 0.0, 2.0, ALU.is_ge, ALU.mult)
                dve.scalar_tensor_tensor(size, g, -1.0, g, ALU.mult, ALU.max).then_inc(s_chain, 1)
                dve.wait_ge(s_chain, start + 1)
                dve.tensor_scalar(size, size, 0.25, None, ALU.max).then_inc(s_chain, 1)
                dve.wait_ge(s_chain, start + 2)
                dve.scalar_tensor_tensor(g, up, -1.0, size, ALU.add, ALU.mult).then_inc(done, 1)

            def modulation():
                dve.wait_ge(s_mod_ps, 1)
                dve.tensor_copy(mod[:, :, :].rearrange("p m b -> p (m b)"), ring[0][:, 0:6 * B])\
                    .then_inc(s_mod, 1)
                dve.wait_ge(s_mod, 1)
                for m in (1, 4):
                    dve.tensor_scalar(mod[:, m, :], mod[:, m, :], 1.0, None, ALU.add)
                at_least(mod[:, 5, :], mod_up[:, :], mod_size[:, :], 0, s_mod)
                dve.wait_ge(s_mod, 2)

            def gate_row():
                dve.wait_ge(s_ga_ps, 1)
                dve.tensor_copy(ga_row[:, :], ps_h[0][0:B, 0, 0:D]).then_inc(s_ga_row, 1)
                dve.wait_ge(s_ga_row, 1)
                at_least(ga_row[:, :], ga_up[:, :], ga_size[:, :], 2, s_ga_row)

            dve.memset(eps_ln[:, :], EPS_LN)
            dve.memset(minus_half[:, :], -0.5).then_inc(s_set, 1)
            dve.memset(b2_f[:, :], 0.0)
            dve.memset(gates_e[:, :].bitcast(F32), 0.0)
            dve.memset(v[:, :, D:D + 1], 1.0).then_inc(s_set, 1)
            dve.memset(v_t[:, 0:PAD], 0.0)
            dve.memset(v_t[:, PAD + S:PAD + S + PAD], 0.0).then_inc(s_set, 1)
            dve.memset(scratch[:, :], 0.0).then_inc(s_store[1], 16)
            schedule(dve, stage, tick)


_OUT = (B, S, D)


def kernel(**inputs):
    import numpy as np
    import concourse.bacc as bacc
    from concourse.bass_utils import run_bass_kernel_spmd as run

    a = {k: np.asarray(v) for k, v in inputs.items()}
    col = lambda v: np.ascontiguousarray(v.reshape(-1, 1))

    freq = (np.float32(1.0) / np.float32(10000.0) ** (np.arange(0, DK, 2, dtype=np.float32) / np.float32(DK)))
    angle = np.arange(S, dtype=np.float32)[:, None] * freq.astype(np.float32)[None, :]
    cos, sin = np.cos(angle), np.sin(angle)
    table = np.stack([np.concatenate([cos, cos], 1), np.concatenate([-sin, sin], 1)])
    rope = np.ascontiguousarray(table.reshape(2, J, P, DK).transpose(2, 0, 1, 3)).astype(np.float32)
    head = np.arange(P) // DK
    scale = float(DK) ** -0.5
    lower = np.tril(np.ones((E, E)), -1).reshape(1, -1).repeat(P, 0)
    consts = np.concatenate([np.eye(P), (head[:, None] == head[None, :]) * scale,
                             (head[:, None] == np.arange(HEADS)[None, :]) * scale, lower], 1)

    arrays = {
        "x": a["L0_attn_hidden_states"],
        "wqkvg": np.concatenate([a[f"L0_attn_W{n}"].T for n in "qkvg"], 1),
        "wo": a["L0_attn_Wo"].T,
        "wmod": a["L0_wmod"],
        "c_t": a["L0_c"].T,
        "lepe": np.concatenate([a["L0_attn_lepe_w"][:, 0, :], col(a["L0_attn_lepe_b"])], 1),
        "w_route": a["L0_ffn_Wg"],
        "b_route": a["L0_ffn_bg"],
        "w1": a["L0_ffn_W1"].transpose(1, 0, 2),
        "b1": a["L0_ffn_b1"].reshape(E, HH, P).transpose(2, 0, 1),
        "w2": a["L0_ffn_W2"].reshape(E, HH, P, D).transpose(2, 0, 1, 3),
        "b2": a["L0_ffn_b2"],
        "rope": rope,
        "consts": consts.astype(np.float32),
    }
    arrays = {k: np.ascontiguousarray(v) for k, v in arrays.items()}
    nc = bacc.Bacc("TRN2", target_bir_lowering=False, num_devices=1)
    aps = {k: nc.dram_tensor(f"in_{k}", v.shape, mybir.dt.from_np(v.dtype), kind="ExternalInput").ap()
           for k, v in arrays.items()}
    out = nc.dram_tensor("out", _OUT, F32, kind="ExternalOutput").ap()
    adaln_moe_kernel(nc, out=out, **aps)
    r = run(nc, [{f"in_{k}": v for k, v in arrays.items()}], core_ids=[0])
    return r.results[0]["out"]
```
